# Optimizing a Trainium2 kernel written in Bass

```python
import numpy as np
import jax
import jax.numpy as jnp

def _softmax(x, axis=-1):
    return jax.nn.softmax(x, axis=axis)

def _gelu(x):
    return jax.nn.gelu(x, approximate=True)

def _silu(x):
    return jax.nn.silu(x)

def _sigmoid(x):
    return jax.nn.sigmoid(x)

def _layernorm(x, axis=-1, eps=1e-05):
    m = jnp.mean(x, axis=axis, keepdims=True)
    v = jnp.var(x, axis=axis, keepdims=True)
    return (x - m) / jnp.sqrt(v + eps)

def _scatter_add(tgt, idx, src, axis=0):
    return tgt.at[idx].add(src)

def _segment_sum(src, seg, n):
    return jax.ops.segment_sum(src, seg, n)
kernel_name = 'mk_macaron_d1_jaxref_r4_ae40e5'

def setup_inputs(seed: int=0):
    np.random.seed(seed)
    _w = jnp.asarray

    def _L0_attn_setup():
        import jax, jax.numpy as jnp
        import numpy as np
        B, L, D, H = (2, 512, 256, 16)
        HD = D // H
        NEG = -1000000000.0

        def sparsemax(z):
            n = z.shape[-1]
            z_sorted = jnp.flip(jnp.sort(z, axis=-1), axis=-1)
            cssv = jnp.cumsum(z_sorted, axis=-1)
            r = jnp.arange(1, n + 1, dtype=z.dtype)
            support = 1.0 + r * z_sorted > cssv
            k = jnp.sum(support, axis=-1, keepdims=True)
            cssv_k = jnp.take_along_axis(cssv, k - 1, axis=-1)
            tau = (cssv_k - 1.0) / k.astype(z.dtype)
            return jnp.maximum(z - tau, 0.0)
        key = jax.random.key(seed)
        ks = jax.random.split(key, 5)
        s = 1.0 / np.sqrt(D)
        return {'x': jax.random.normal(ks[0], (B, L, D), dtype=jnp.float32), 'Wq': jax.random.normal(ks[1], (D, D), dtype=jnp.float32) * s, 'Wk': jax.random.normal(ks[2], (D, D), dtype=jnp.float32) * s, 'Wv': jax.random.normal(ks[3], (D, D), dtype=jnp.float32) * s, 'Wo': jax.random.normal(ks[4], (D, D), dtype=jnp.float32) * s}
    _L0_attn_in = _L0_attn_setup()

    def _L0_ffn_setup():
        import jax, jax.numpy as jnp
        import numpy as np
        DIM = 256

        def _reference_tuple_inner(x, W_r, W_k, W_v, mu_r, mu_k):
            B, T, C = x.shape
            x_prev = jnp.concatenate([jnp.zeros((B, 1, C), x.dtype), x[:, :-1, :]], axis=1)
            xr = mu_r * x + (1.0 - mu_r) * x_prev
            xk = mu_k * x + (1.0 - mu_k) * x_prev
            r = jax.nn.sigmoid(jnp.einsum('btc,dc->btd', xr, W_r))
            k = jnp.einsum('btc,dc->btd', xk, W_k)
            k_act = jnp.square(jax.nn.relu(k))
            out = r * jnp.einsum('btc,dc->btd', k_act, W_v)
            new_state = x[:, -1, :]
            return (out, new_state)
        key = jax.random.key(seed)
        ks = jax.random.split(key, 6)
        B, T, C = (8, 512, DIM)
        x = jax.random.normal(ks[0], (B, T, C), dtype=jnp.float32)
        s = 1.0 / np.sqrt(C)
        W_r = jax.random.uniform(ks[1], (C, C), jnp.float32, -s, s)
        W_k = jax.random.uniform(ks[2], (C, C), jnp.float32, -s, s)
        W_v = jax.random.uniform(ks[3], (C, C), jnp.float32, -s, s)
        mu_r = jax.random.uniform(ks[4], (C,), jnp.float32)
        mu_k = jax.random.uniform(ks[5], (C,), jnp.float32)
        return {'x': x, 'W_r': W_r, 'W_k': W_k, 'W_v': W_v, 'mu_r': mu_r, 'mu_k': mu_k}
    _L0_ffn_in = _L0_ffn_setup()
    _d = {'L0_attn_x': _L0_attn_in['x'], 'L0_attn_Wq': _L0_attn_in['Wq'], 'L0_attn_Wk': _L0_attn_in['Wk'], 'L0_attn_Wv': _L0_attn_in['Wv'], 'L0_attn_Wo': _L0_attn_in['Wo'], 'L0_ffn_W_r': _L0_ffn_in['W_r'], 'L0_ffn_W_k': _L0_ffn_in['W_k'], 'L0_ffn_W_v': _L0_ffn_in['W_v'], 'L0_ffn_mu_r': _L0_ffn_in['mu_r'], 'L0_ffn_mu_k': _L0_ffn_in['mu_k']}
    _x0 = _d['L0_attn_x']
    _d['L0_attn_x'] = jax.random.normal(jax.random.fold_in(jax.random.key(seed), 1), (8, 1024, 256), dtype=_x0.dtype)
    del _x0
    return _d

def reference(L0_attn_x, L0_attn_Wq, L0_attn_Wk, L0_attn_Wv, L0_attn_Wo, L0_ffn_W_r, L0_ffn_W_k, L0_ffn_W_v, L0_ffn_mu_r, L0_ffn_mu_k):

    def _L0_attn_ref(x, Wq, Wk, Wv, Wo):
        import jax, jax.numpy as jnp
        import numpy as np
        B, L, D, H = (2, 512, 256, 16)
        HD = D // H
        NEG = -1000000000.0

        def sparsemax(z):
            n = z.shape[-1]
            z_sorted = jnp.flip(jnp.sort(z, axis=-1), axis=-1)
            cssv = jnp.cumsum(z_sorted, axis=-1)
            r = jnp.arange(1, n + 1, dtype=z.dtype)
            support = 1.0 + r * z_sorted > cssv
            k = jnp.sum(support, axis=-1, keepdims=True)
            cssv_k = jnp.take_along_axis(cssv, k - 1, axis=-1)
            tau = (cssv_k - 1.0) / k.astype(z.dtype)
            return jnp.maximum(z - tau, 0.0)
        b, l, d = x.shape

        def proj(W):
            return jnp.einsum('bld,ed->ble', x, W).reshape(b, l, H, HD).transpose(0, 2, 1, 3)
        q, k, v = (proj(Wq), proj(Wk), proj(Wv))
        scores = jnp.einsum('bhqd,bhkd->bhqk', q, k) / np.sqrt(HD)
        causal = jnp.tril(jnp.ones((l, l), dtype=bool))
        scores = jnp.where(causal, scores, NEG)
        attn = sparsemax(scores)
        out = jnp.einsum('bhqk,bhkd->bhqd', attn, v)
        out = out.transpose(0, 2, 1, 3).reshape(b, l, d)
        return jnp.einsum('bld,ed->ble', out, Wo)

    def _L0_ffn_ref(x, W_r, W_k, W_v, mu_r, mu_k):
        import jax, jax.numpy as jnp
        import numpy as np
        DIM = 256

        def _reference_tuple_inner(x, W_r, W_k, W_v, mu_r, mu_k):
            B, T, C = x.shape
            x_prev = jnp.concatenate([jnp.zeros((B, 1, C), x.dtype), x[:, :-1, :]], axis=1)
            xr = mu_r * x + (1.0 - mu_r) * x_prev
            xk = mu_k * x + (1.0 - mu_k) * x_prev
            r = jax.nn.sigmoid(jnp.einsum('btc,dc->btd', xr, W_r))
            k = jnp.einsum('btc,dc->btd', xk, W_k)
            k_act = jnp.square(jax.nn.relu(k))
            out = r * jnp.einsum('btc,dc->btd', k_act, W_v)
            new_state = x[:, -1, :]
            return (out, new_state)
        return _reference_tuple_inner(x, W_r, W_k, W_v, mu_r, mu_k)[0]
    x = L0_attn_x
    x = x + 0.5 * _L0_ffn_ref(_layernorm(x, axis=-1), L0_ffn_W_r, L0_ffn_W_k, L0_ffn_W_v, L0_ffn_mu_r, L0_ffn_mu_k)
    x = x + _L0_attn_ref(_layernorm(x, axis=-1), L0_attn_Wq, L0_attn_Wk, L0_attn_Wv, L0_attn_Wo)
    x = x + 0.5 * _L0_ffn_ref(_layernorm(x, axis=-1), L0_ffn_W_r, L0_ffn_W_k, L0_ffn_W_v, L0_ffn_mu_r, L0_ffn_mu_k)
    return x

_drawn_inputs = setup_inputs


def setup_inputs(seed=0):
    import zlib

    import numpy as np

    out = dict(_drawn_inputs(seed))
    spreads = {}
    factors = {'L0_ffn_mu_r': 5.08}
    for name, (base, spread) in spreads.items():
        noise = np.random.default_rng([zlib.crc32(name.encode()), seed]).standard_normal(out[name].shape)
        drawn = base * np.exp(spread * noise) if base else spread * noise
        out[name] = jnp.asarray(drawn.astype(out[name].dtype))
    for name, factor in factors.items():
        out[name] = (out[name] * factor).astype(out[name].dtype)
    return out
```

```python
from contextlib import ExitStack

import concourse.bass as bass
from concourse import mybir

ALU = mybir.AluOpType
ACT = mybir.ActivationFunctionType
AX = mybir.AxisListType
F32 = mybir.dt.float32
BF16 = mybir.dt.bfloat16
I32 = mybir.dt.int32

P = 128
BATCH, T, D, H = 8, 1024, 256, 16
HD = D // H
NT = T // P
C = D // P
UH = 4
UNITS = H // UH
PAIRS = NT // 2
PUS = UNITS * PAIRS
HT = 2 * UH
ROWW = (NT + 1) * P
TOP = 16
MASKED = -1.0e30
EPS = 1e-5
G = 2
TH = T // G
QPART = [0, 0, 1, 1, 0, 2]
KPART = [0, 1, 0, 1, 2, 0]
SROWS = HD * len(QPART)
TROWS = SROWS + 3
ROUNDS = 16


def segments(qt):
    w = 64 if qt == 0 else 128
    n = (qt + 1) * P
    return [(a, min(w, n - a)) for a in range(0, n, w)]


def row_chunks(p):
    out = []
    for qt, base in ((p, 0), (NT - 1 - p, (p + 1) * P)):
        n = (qt + 1) * P
        out += [(qt, a, min(512, n - a), base + a) for a in range(0, n, 512)]
    return out


STEPS = [(s, j, max(TH * s, P * j)) for s in range(G) for j in range(NT * (s + 1) // G)]
THIRDS = {1: STEPS[0:5], 2: STEPS[5:8], 3: STEPS[8:12]}
CHUNKS = 3
SLOTS = PUS + PAIRS


PER_UNIT = UH * len(STEPS)


def quarters(steps):
    return [steps[len(steps) * i // UH:len(steps) * (i + 1) // UH] for i in range(UH)]


def slot_steps(n):
    u = n // PAIRS - 1
    if n < PAIRS or n % PAIRS == 0:
        return None, [[], [], [], []]
    return u, quarters(THIRDS[n % PAIRS])


def misc_plan():
    plan = []

    def ffn(f):
        for g in range(G):
            plan.extend((("yT", 2 * f if f == 0 else 2, g, tp, c), "act") for tp in range(2) for c in range(C))
            plan.extend((("r", f, g, t), "act") for t in range(4))
            plan.extend((("k", f, g, m, tp), "act") for tp in range(2) for m in range(C))
            plan.extend((("v", f, g, t), "dve") for t in range(4))

    ffn(0)
    for g in range(G):
        plan.extend((("yT", 1, g, tp, c), "act") for tp in range(2) for c in range(C))
    for n in range(T // 256):
        plan.extend((("qk", w, m, n), "dve") for w in range(2) for m in range(C))
    plan.extend((("val", t), "act") for t in range(NT))
    for n in range(SLOTS):
        if 1 <= n <= PUS:
            plan.append((("flag", n - 1), "dve"))
        if n >= PAIRS and n % PAIRS == 1:
            plan.append((("tau", n // PAIRS - 1), "act"))
    plan.extend((("o", t), "dve") for t in range(NT))
    ffn(1)
    return plan


PLAN = misc_plan()
TASK = {key: i for i, (key, _) in enumerate(PLAN)}
EMPTIED = {}
for _i, (_key, _eng) in enumerate(PLAN):
    EMPTIED[_key] = sum(e == _eng for _, e in PLAN[:_i + 1])
TASKS = len(PLAN)
TASKS_BY = {e: sum(x == e for _, x in PLAN) for e in ("act", "dve")}
CHAIN = 606


def macaron(nc, x_in, wr, wk, wv, mur, muk, wq, wkk, wvv, wo, out):
    with ExitStack() as ctx:
        def sb(name, shape, dt=F32):
            return ctx.enter_context(nc.sbuf_tensor(name, shape, dt))

        def ps(name, shape, dt=F32):
            return ctx.enter_context(nc.psum_tensor(name, shape, dt))

        def sem(name):
            return ctx.enter_context(nc.semaphore(name))

        w_sb = {n: sb("w_" + n, [P, C, D]) for n in ("r", "k", "v", "q", "kk", "vv")}
        wo_sb = sb("wo_sb", [P, UNITS, D])
        mu_sb = sb("mu_sb", [P, 2, C])
        ident = sb("ident", [P, P])
        ident_b = sb("ident_b", [P, P], BF16)
        mask_row = sb("mask_row", [P, P], BF16)
        mask_col = sb("mask_col", [P, P], BF16)
        ones_b = sb("ones_b", [P, 1], BF16)
        carry = sb("carry", [P, HT, TOP])
        inv_rank = sb("inv_rank", [P, HT, TOP])
        eps_sb = sb("eps_sb", [P, 1])
        zero_sb = sb("zero_sb", [P, C])

        X = sb("X", [P, NT, D])
        stats = sb("stats", [P, 4, 6])
        mv = sb("mv", [P, 4, 2])
        sd = sb("sd", [P, 4])
        rstd = sb("rstd", [P, 4])
        ytok = sb("ytok", [P, 4, D])
        yT = sb("yT", [P, C, TH + 1])
        xr = sb("xr", [P, C, TH])
        xk = sb("xk", [P, C, TH])
        upd = sb("upd", [P, 2, D])
        y2T = sb("y2T", [P, C, T])
        V = sb("V", [P, NT, D])
        part = [[sb(f"part_{w}{i}", [P, C, T], BF16) for i in range(3)] for w in "qk"]
        res = sb("res", [P, 2, 256])
        stack = [[sb(f"stack_{w}{i}", [TROWS, UH, T], BF16) for i in range(2)] for w in "qk"]
        OT = sb("OT", [P, UNITS, T])

        score = [sb(f"score{i}", [P, UH, ROWW]) for i in range(2)]
        cand = sb("cand", [P, HT, 64])
        rest = sb("rest", [P, HT, 64])
        best = sb("best", [P, HT, TOP])
        cum = sb("cum", [P, HT, TOP])
        edge = sb("edge", [P, UH, 2])
        flag = sb("flag", [P, HT + 1])
        flag_b = sb("flag_b", [P, 2, HT + 1], BF16)
        flag_n = sb("flag_n", [1, HT + 1], I32)
        tau = [sb(f"tau{i}", [P, UH, NT]) for i in range(2)]
        ntau = sb("ntau", [P, 2, UH * NT])
        tau_part = sb("tau_part", [P, 3, UH * NT], BF16)
        tauT = sb("tauT", [3 * UH * NT, P], BF16)
        n_tau = sb("n_tau", [P, 1])
        n_sum = sb("n_sum", [P, 1])
        n_cnt = sb("n_cnt", [P, 2])
        n_inv = sb("n_inv", [P, 1])
        n_square = sb("n_square", [P, 32])
        n_turned = sb("n_turned", [P, 32])
        n_left = sb("n_left", [P, 1], I32)
        probs = sb("probs", [P, 2, UH, TH])
        junk = sb("junk", [P, T], BF16)

        row_ps = ps("row_ps", [P, 2, 512])
        col_ps = ps("col_ps", [P, 3, 512])
        o_ps = ps("o_ps", [P, 512])
        misc_ps = ps("misc_ps", [P, 2, 512])

        w_loaded, pads_zero, consts = sem("w_loaded"), sem("pads_zero"), sem("consts")
        o_zeroed = sem("o_zeroed")
        x_loaded, x_stored = sem("x_loaded"), sem("x_stored")
        ln_stats, ln_sd, y_ready = sem("ln_stats"), sem("ln_sd"), sem("y_ready")
        misc_filled, misc_act, misc_dve = sem("misc_filled"), sem("misc_act"), sem("misc_dve")
        diff_ready, xr_ready, xk_ready = sem("diff_ready"), sem("xr_ready"), sem("xk_ready")
        hidden_ready, x_added = sem("hidden_ready"), sem("x_added")
        hi_ready, mid_ready, lo_ready = sem("hi_ready"), sem("mid_ready"), sem("lo_ready")
        stack_loaded = [sem("stack_loaded0"), sem("stack_loaded1")]
        unit_scored = sem("unit_scored")
        row_filled, row_copied = sem("row_filled"), sem("row_copied")
        flags_ready, pu_settled = sem("flags_ready"), sem("pu_settled")
        tau_split, tau_loaded = sem("tau_split"), sem("tau_loaded")
        split_chain = sem("split_chain")
        col_filled, probs_ready, pv_done = sem("col_filled"), sem("probs_ready"), sem("pv_done")
        o_copied = sem("o_copied")
        dve_chain = sem("dve_chain")
        wait_kept = sem("wait_kept")

        x_v = x_in.rearrange("b (t p) d -> b p t d", p=P)
        out_v = out.rearrange("b (t p) d -> b p t d", p=P)

        ctx.enter_context(nc.allow_low_precision("the operands are split exactly into bfloat16 parts"))
        block = ctx.enter_context(nc.Block())
        PU_ROWS = UH * CHUNKS

        @block.sync
        def _(sp):
            for t, src in ((w_sb["r"], wr), (w_sb["k"], wk), (w_sb["v"], wv), (w_sb["q"], wq),
                           (w_sb["kk"], wkk), (w_sb["vv"], wvv)):
                sp.dma_start(t[:, :, :], src).then_inc(w_loaded, 16)
            sp.dma_start(mu_sb[:, 0, :], mur).then_inc(w_loaded, 16)
            sp.dma_start(mu_sb[:, 1, :], muk).then_inc(w_loaded, 16)
            sp.wait_ge(pads_zero, 1)
            for h in range(UH):
                sp.dma_start(wo_sb[32 * h:32 * h + HD, :, :], wo[:, h, :, :]).then_inc(w_loaded, 16)
            with sp.Fori(0, BATCH) as b:
                sp.dma_start(X[:, :, :], x_v[bass.ds(b, 1)].rearrange("o p t d -> p (o t) d")).then_inc(x_loaded, 16)
                sp.wait_ge(lo_ready, b * 16 + 16)
                sp.sem_inc(wait_kept, 1)
                for n in range(SLOTS):
                    if n % PAIRS == 0 and n < PUS:
                        u = n // PAIRS
                        if u >= 2:
                            sp.wait_ge(unit_scored, b * UNITS + u - 1)
                        rows = slice(64 * (u % 2), 64 * (u % 2) + 64)
                        for w, parts in ((0, QPART), (1, KPART)):
                            for j, i in enumerate(parts):
                                sp.dma_start(stack[w][u % 2][HD * j:HD * (j + 1), :, :],
                                             part[w][i][rows, u // 2, :]).then_inc(stack_loaded[u % 2], 16)
                    if n >= PAIRS and n % PAIRS == 1:
                        u = n // PAIRS - 1
                        sp.wait_ge(misc_act, b * TASKS_BY["act"] + EMPTIED[("tau", u)])
                        sp.dma_start(stack[0][u % 2][SROWS:TROWS, :, :], tauT[:, :]).then_inc(tau_loaded, 16)
                sp.wait_ge(x_added, b * 3 * NT + 3 * NT)
                sp.sem_inc(wait_kept, 1)
                sp.dma_start(out_v[bass.ds(b, 1)].rearrange("o p t d -> p (o t) d"), X[:, :, :]).then_inc(x_stored, 16)
                sp.wait_ge(x_stored, b * 16 + 16)
                sp.sem_inc(wait_kept, 1)

        @block.gpsimd
        def _(pool):
            pool.memset(wo_sb[:, :, :], 0.0).then_inc(pads_zero, 1)
            pool.memset(ident[:, :], 0.0).then_inc(split_chain, 1)
            pool.memset(ident_b[:, :], 0.0).then_inc(split_chain, 1)
            pool.memset(mask_row[:, :], 0.0).then_inc(split_chain, 1)
            pool.memset(mask_col[:, :], 0.0).then_inc(split_chain, 1)
            pool.memset(carry[:, :, :], 1.0).then_inc(split_chain, 1)
            pool.memset(ones_b[:, :], 1.0)
            pool.memset(eps_sb[:, :], EPS)
            pool.memset(zero_sb[:, :], 0.0)
            pool.memset(n_square[:, :], 0.0)
            for r in range(TOP):
                pool.memset(inv_rank[:, :, r:r + 1], 1.0 / (r + 1))
            pool.wait_ge(split_chain, 5)
            for t in (ident, ident_b):
                pool.affine_select(out=t[:, :], in_=t[:, :], compare_op=ALU.not_equal, fill=1.0, base=0,
                                   pattern=[[-1, P]], channel_multiplier=1)
            pool.affine_select(out=mask_row[:, :], in_=mask_row[:, :], compare_op=ALU.is_ge, fill=MASKED, base=0,
                               pattern=[[-1, P]], channel_multiplier=1)
            pool.affine_select(out=mask_col[:, :], in_=mask_col[:, :], compare_op=ALU.is_ge, fill=MASKED, base=0,
                               pattern=[[1, P]], channel_multiplier=-1)
            pool.memset(carry[:, :, 0:1], 0.0)
            pool.drain().then_inc(consts, 1)

            def ffn(b, f):
                for g in range(G):
                    pool.wait_ge(misc_act, b * TASKS_BY["act"] + EMPTIED[("yT", 2 * f, g, 1, C - 1)])
                    for c in range(C):
                        ins = pool.tensor_tensor(xk[:, c, :], yT[:, c, 1:TH + 1], yT[:, c, 0:TH], ALU.subtract)
                        if c == C - 1:
                            ins.then_inc(diff_ready, 1)
                    pool.wait_ge(misc_act, b * TASKS_BY["act"] + EMPTIED[("k", f, g, C - 1, 1)])
                    for m in range(C):
                        ins = pool.tensor_tensor(xr[:, m, :], xr[:, m, :], xr[:, m, :], ALU.mult)
                        if m == C - 1:
                            ins.then_inc(hidden_ready, 1)

            with pool.Fori(0, BATCH) as b:
                ffn(b, 0)
                for n in range(T // 256):
                    for w in range(2):
                        for m in range(C):
                            i = 4 * n + 2 * w + m
                            pool.wait_ge(mid_ready, b * 16 + i + 1)
                            pool.tensor_tensor(part[w][2][:, m, 256 * n:256 * n + 256], res[:, i % 2, :],
                                               part[w][1][:, m, 256 * n:256 * n + 256],
                                               ALU.subtract).then_inc(lo_ready, 1)
                for u in range(UNITS):
                    pool.wait_ge(pu_settled, b * PUS + PAIRS * (u + 1))
                    if u:
                        pool.wait_ge(misc_filled, b * TASKS + TASK[("tau", u - 1)] + 1)
                    pool.sem_inc(wait_kept, 1)
                    t = tau[u % 2][:, :, :].rearrange("p h q -> p (h q)")
                    base = b * UNITS * 5 + (5 * u + 5)
                    pool.tensor_scalar(ntau[:, 0, :], t, -1.0, 0.0, ALU.mult, ALU.add).then_inc(split_chain, 1)
                    pool.wait_ge(split_chain, base + 1)
                    pool.sem_inc(wait_kept, 1)
                    pool.tensor_copy(tau_part[:, 0, :], ntau[:, 0, :]).then_inc(split_chain, 1)
                    pool.wait_ge(split_chain, base + 2)
                    pool.tensor_tensor(ntau[:, 1, :], ntau[:, 0, :], tau_part[:, 0, :], ALU.subtract).then_inc(split_chain, 1)
                    pool.wait_ge(split_chain, base + 3)
                    pool.sem_inc(wait_kept, 1)
                    pool.tensor_copy(tau_part[:, 1, :], ntau[:, 1, :]).then_inc(split_chain, 1)
                    pool.wait_ge(split_chain, base + 4)
                    pool.tensor_tensor(tau_part[:, 2, :], ntau[:, 1, :], tau_part[:, 1, :], ALU.subtract).then_inc(split_chain, 1)
                    pool.wait_ge(split_chain, base + 5)
                    pool.sem_inc(tau_split, 1)
                ffn(b, 1)

        @block.tensor
        def _(pe):
            pe.wait_ge(w_loaded, 12 * 16)
            pe.wait_ge(consts, 1)
            pe.wait_ge(o_zeroed, 1)

            def open_task(b, key):
                k = TASK[key]
                before, eng = PLAN[(k - 2) % TASKS]
                s = misc_act if eng == "act" else misc_dve
                if k >= 2:
                    pe.wait_ge(s, b * TASKS_BY[eng] + EMPTIED[before])
                return misc_ps[:, k % 2, 0:256]

            def turn(b, layer, g):
                for tp in range(2):
                    pe.wait_ge(y_ready, b * 24 + 8 * layer + 4 * g + 2 * tp + 2)
                    for c in range(C):
                        m = open_task(b, ("yT", layer, g, tp, c))
                        for i in range(2):
                            ins = pe.transpose(m[:, P * i:P * (i + 1)], ytok[:, 2 * tp + i, P * c:P * (c + 1)], ident[:, :])
                        ins.then_inc(misc_filled, 1)

            def product(m, left, right):
                for c in range(len(left)):
                    ins = pe.matmul(m, left[c], right[c], start=(c == 0), stop=(c == len(left) - 1))
                ins.then_inc(misc_filled, 1)

            def ffn(b, f):
                for g in range(G):
                    turn(b, 2 * f, g)
                    pe.wait_ge(xr_ready, b * 4 + 2 * f + g + 1)
                    for t in range(4):
                        m = open_task(b, ("r", f, g, t))
                        product(m, [xr[:, c, P * t:P * (t + 1)] for c in range(C)], [w_sb["r"][:, c, :] for c in range(C)])
                    pe.wait_ge(xk_ready, b * 4 + 2 * f + g + 1)
                    for tp in range(2):
                        for mm in range(C):
                            m = open_task(b, ("k", f, g, mm, tp))
                            product(m, [w_sb["k"][:, c, P * mm:P * (mm + 1)] for c in range(C)],
                                    [xk[:, c, 256 * tp:256 * tp + 256] for c in range(C)])
                    pe.wait_ge(hidden_ready, b * 4 + 2 * f + g + 1)
                    for t in range(4):
                        m = open_task(b, ("v", f, g, t))
                        product(m, [xr[:, c, P * t:P * (t + 1)] for c in range(C)], [w_sb["v"][:, c, :] for c in range(C)])

            def scores_head(b, n, hh):
                u, p = n // PAIRS, n % PAIRS
                q, k = stack[0][u % 2], stack[1][u % 2]
                for i, (qt, a, w, _) in enumerate(row_chunks(p)):
                    at = PU_ROWS * n + CHUNKS * hh + i
                    if at >= 2:
                        pe.wait_ge(row_copied, b * PU_ROWS * PUS + at - 1)
                    bank = row_ps[:, at % 2, :]
                    last = a + w == (qt + 1) * P
                    ins = pe.matmul(bank[:, 0:w], q[0:SROWS, hh, P * qt:P * (qt + 1)], k[0:SROWS, hh, a:a + w],
                                    start=True, stop=not last)
                    if last:
                        ins = pe.matmul(bank[:, w - P:w], ident_b[:, :], mask_row[:, :], start=False, stop=True)
                    ins.then_inc(row_filled, 1)

            def step_scores(b, u, k):
                s, j, q0 = STEPS[k]
                w = TH * (s + 1) - q0
                q, kk = stack[0][u % 2], stack[1][u % 2]
                diagonal = P * j >= TH * s
                for hh in range(UH):
                    at = PER_UNIT * u + UH * k + hh
                    if at >= 3:
                        pe.wait_ge(probs_ready, b * UNITS * PER_UNIT + at - 2)
                    ins = pe.matmul(col_ps[:, at % 3, 0:w], kk[0:TROWS, hh, P * j:P * (j + 1)],
                                    q[0:TROWS, hh, q0:q0 + w], start=True, stop=not diagonal)
                    if diagonal:
                        ins = pe.matmul(col_ps[:, at % 3, 0:P], ident_b[:, :], mask_col[:, :], start=False, stop=True)
                    ins.then_inc(col_filled, 1)
                if k == len(STEPS) - 1:
                    pe.wait_ge(col_filled, b * UNITS * PER_UNIT + PER_UNIT * (u + 1))
                    pe.sem_inc(unit_scored, 1)

            def step_values(b, u, k):
                s, j, q0 = STEPS[k]
                w = TH * (s + 1) - q0
                if j == 0 and (u, s) != (0, 0):
                    pe.wait_ge(o_copied, b * 8 + 2 * u + s)
                pe.wait_ge(probs_ready, b * UNITS * PER_UNIT + PER_UNIT * u + UH * (k + 1))
                for hh in range(UH):
                    col = (UH * u + hh) * HD
                    ins = pe.matmul(o_ps[32 * hh:32 * hh + HD, TH - w:TH], V[:, j, col:col + HD],
                                    probs[:, k % 2, hh, 0:w], start=(j == 0), stop=(P * (j + 1) == TH * (s + 1)),
                                    skip_group_check=True)
                ins.then_inc(pv_done, 1)

            with pe.Fori(0, BATCH) as b:
                ffn(b, 0)
                for g in range(G):
                    turn(b, 1, g)
                for n in range(T // 256):
                    pe.wait_ge(misc_act, b * TASKS_BY["act"] + EMPTIED[("yT", 1, n // 2, n % 2, C - 1)])
                    for w, name in enumerate(("q", "kk")):
                        for mm in range(C):
                            m = open_task(b, ("qk", w, mm, n))
                            product(m, [w_sb[name][:, c, P * mm:P * (mm + 1)] for c in range(C)],
                                    [y2T[:, c, 256 * n:256 * n + 256] for c in range(C)])
                for t in range(NT):
                    m = open_task(b, ("val", t))
                    product(m, [y2T[:, c, P * t:P * (t + 1)] for c in range(C)], [w_sb["vv"][:, c, :] for c in range(C)])
                pe.wait_ge(misc_act, b * TASKS_BY["act"] + EMPTIED[("val", NT - 1)])
                for n in range(SLOTS):
                    u, steps = slot_steps(n)
                    if n < PUS and n % PAIRS == 0:
                        uu = n // PAIRS
                        pe.wait_ge(stack_loaded[uu % 2], b * 384 + 192 * (uu // 2 + 1))
                    for hh in range(UH):
                        if n < PUS:
                            scores_head(b, n, hh)
                        if hh == 0 and 1 <= n <= PUS:
                            m = open_task(b, ("flag", n - 1))
                            pe.wait_ge(flags_ready, b * PUS + n)
                            pe.matmul(m[0:1, 0:HT + 1], ones_b[:, :], flag_b[:, (n - 1) % 2, :], start=True,
                                      stop=True).then_inc(misc_filled, 1)
                        if hh == 0 and n >= PAIRS and n % PAIRS == 1:
                            m = open_task(b, ("tau", u)).bitcast(BF16)
                            pe.wait_ge(tau_split, b * UNITS + u + 1)
                            pe.transpose(m[0:3 * UH * NT, 0:P], tau_part[:, :, :].rearrange("p a q -> p (a q)"),
                                         ident_b[:, :]).then_inc(misc_filled, 1)
                            pe.wait_ge(tau_loaded, b * 64 + 16 * (u + 1))
                        for st in steps[hh]:
                            k = STEPS.index(st)
                            step_scores(b, u, k)
                            if k:
                                step_values(b, u, k - 1)
                            if k == len(STEPS) - 1:
                                step_values(b, u, k)
                pe.wait_ge(o_copied, b * 8 + 8)
                for t in range(NT):
                    m = open_task(b, ("o", t))
                    product(m, [OT[:, u, P * t:P * (t + 1)] for u in range(UNITS)], [wo_sb[:, u, :] for u in range(UNITS)])
                ffn(b, 1)

        @block.scalar
        def _(act):
            act.wait_ge(consts, 1)

            def emptying(b, key):
                act.wait_ge(misc_filled, b * TASKS + TASK[key] + 1)
                return misc_ps[:, TASK[key] % 2, 0:256]

            def deviations(b, layer, g):
                act.wait_ge(ln_stats, b * 6 + 2 * layer + g + 1)
                act.activation(sd[:, :], mv[:, :, 1], ACT.Sqrt, bias=eps_sb[:, 0:1]).then_inc(ln_sd, 1)

            def turned(b, f, g):
                layer = 2 * f
                for tp in range(2):
                    for c in range(C):
                        m = emptying(b, ("yT", layer, g, tp, c))
                        if tp == 0 and c == 0:
                            if (f, g) != (0, 0):
                                act.wait_ge(xk_ready, b * 4 + 2 * f + g)
                            if g == 0:
                                ins = act.activation(yT[:, :, 0], zero_sb[:, :], ACT.Copy)
                            else:
                                ins = act.activation(yT[:, :, 0], yT[:, :, TH], ACT.Copy)
                            act.drain()
                        act.activation(yT[:, c, 1 + 256 * tp:257 + 256 * tp], m, ACT.Copy).then_inc(misc_act, 1)

            def ffn(b, f):
                for g in range(G):
                    deviations(b, 2 * f, g)
                    turned(b, f, g)
                    for t in range(4):
                        m = emptying(b, ("r", f, g, t))
                        act.activation(ytok[:, t, :], m, ACT.Sigmoid).then_inc(misc_act, 1)
                    for tp in range(2):
                        for mm in range(C):
                            m = emptying(b, ("k", f, g, mm, tp))
                            act.activation(xr[:, mm, 256 * tp:256 * tp + 256], m, ACT.Relu).then_inc(misc_act, 1)

            def copy_head(b, n, hh):
                if hh == 0:
                    if n >= 2:
                        act.wait_ge(pu_settled, b * PUS + n - 1)
                for i, (qt, a, w, place) in enumerate(row_chunks(n % PAIRS)):
                    at = PU_ROWS * n + CHUNKS * hh + i
                    act.wait_ge(row_filled, b * PU_ROWS * PUS + at + 1)
                    act.activation(score[n % 2][:, hh, place:place + w], row_ps[:, at % 2, 0:w],
                                   ACT.Copy).then_inc(row_copied, 1)

            def step_probs(b, u, k):
                s, j, q0 = STEPS[k]
                w = TH * (s + 1) - q0
                if 12 * u + k >= 2:
                    act.wait_ge(pv_done, b * 48 + 12 * u + k - 1)
                for hh in range(UH):
                    at = PER_UNIT * u + UH * k + hh
                    act.wait_ge(col_filled, b * UNITS * PER_UNIT + at + 1)
                    act.activation(probs[:, k % 2, hh, 0:w], col_ps[:, at % 3, 0:w], ACT.Relu).then_inc(probs_ready, 1)

            def output_half(b, u, s):
                act.wait_ge(pv_done, b * 48 + 12 * u + (4 if s == 0 else 12))
                act.activation(OT[:, u, TH * s:TH * (s + 1)], o_ps[:, :], ACT.Copy).then_inc(o_copied, 1)

            with act.Fori(0, BATCH) as b:
                ffn(b, 0)
                for g in range(G):
                    deviations(b, 1, g)
                    for tp in range(2):
                        for c in range(C):
                            m = emptying(b, ("yT", 1, g, tp, c))
                            at = TH * g + 256 * tp
                            act.activation(y2T[:, c, at:at + 256], m, ACT.Copy).then_inc(misc_act, 1)
                for n in range(T // 256):
                    for w in range(2):
                        for m_ in range(C):
                            i = 4 * n + 2 * w + m_
                            at = slice(256 * n, 256 * n + 256)
                            m = emptying(b, ("qk", w, m_, n))
                            act.activation(part[w][0][:, m_, at], m, ACT.Copy,
                                           scale=0.25 if w == 0 else 1.0).then_inc(hi_ready, 1)
                            act.wait_ge(misc_dve, b * TASKS_BY["dve"] + EMPTIED[("qk", w, m_, n)])
                            act.activation(part[w][1][:, m_, at], res[:, i % 2, :], ACT.Copy).then_inc(mid_ready, 1)
                for t in range(NT):
                    m = emptying(b, ("val", t))
                    act.activation(V[:, t, :], m, ACT.Copy).then_inc(misc_act, 1)
                for n in range(SLOTS):
                    u, steps = slot_steps(n)
                    for hh in range(UH):
                        if n < PUS:
                            copy_head(b, n, hh)
                        if hh == 0 and n >= PAIRS and n % PAIRS == 1:
                            m = emptying(b, ("tau", u)).bitcast(BF16)
                            if u:
                                act.wait_ge(tau_loaded, b * 64 + 16 * u)
                            act.activation(tauT[:, :], m[0:3 * UH * NT, 0:P], ACT.Copy).then_inc(misc_act, 1)
                        for st in steps[hh]:
                            k = STEPS.index(st)
                            step_probs(b, u, k)
                            if k == 5:
                                output_half(b, u, 0)
                            if k == len(STEPS) - 1:
                                output_half(b, u, 1)
                ffn(b, 1)

        @block.vector
        def _(dve):
            chain = [0]
            for i in range(2):
                dve.memset(stack[1][i][SROWS:TROWS, :, :], 1.0)
            dve.memset(o_ps[:, :], 0.0).then_inc(o_zeroed, 1)
            dve.wait_ge(consts, 1)
            dve.wait_ge(w_loaded, 12 * 16)

            def step(ins):
                chain[0] += 1
                ins.then_inc(dve_chain, 1)
                return chain[0]

            def settled(b, k):
                dve.wait_ge(dve_chain, b * CHAIN + k)

            def apart():
                dve.sem_inc(wait_kept, 1)

            def normalise(b, layer, g):
                for t in range(4):
                    k = step(dve.bn_stats(stats[:, t, :], X[:, 4 * g + t, :]))
                settled(b, k)
                apart()
                for t in range(4):
                    ins = dve.bn_aggr(mv[:, t, :], stats[:, t, :])
                ins.then_inc(ln_stats, 1)
                dve.wait_ge(ln_sd, b * 6 + 2 * layer + g + 1)
                settled(b, step(dve.reciprocal(rstd[:, :], sd[:, :])))
                for t in range(4):
                    dve.tensor_scalar(ytok[:, t, :], X[:, 4 * g + t, :], mv[:, t, 0:1], rstd[:, t:t + 1],
                                      ALU.subtract, ALU.mult).then_inc(y_ready, 1)

            def ffn(b, f, added):
                for g in range(G):
                    normalise(b, 2 * f, g)
                    dve.wait_ge(diff_ready, b * 4 + 2 * f + g + 1)
                    for c in range(C):
                        ins = dve.scalar_tensor_tensor(out=xr[:, c, :], in0=xk[:, c, :], scalar=mu_sb[:, 0, c:c + 1],
                                                       in1=yT[:, c, 0:TH], op0=ALU.mult, op1=ALU.add)
                    ins.then_inc(xr_ready, 1)
                    dve.wait_ge(xr_ready, b * 4 + 2 * f + g + 1)
                    for c in range(C):
                        ins = dve.scalar_tensor_tensor(out=xk[:, c, :], in0=xk[:, c, :], scalar=mu_sb[:, 1, c:c + 1],
                                                       in1=yT[:, c, 0:TH], op0=ALU.mult, op1=ALU.add)
                    ins.then_inc(xk_ready, 1)
                    for t in range(4):
                        key = ("v", f, g, t)
                        dve.wait_ge(misc_filled, b * TASKS + TASK[key] + 1)
                        dve.wait_ge(misc_act, b * TASKS_BY["act"] + EMPTIED[("r", f, g, t)])
                        dve.scalar_tensor_tensor(out=upd[:, t % 2, :], in0=misc_ps[:, TASK[key] % 2, 0:256], scalar=0.5,
                                                 in1=ytok[:, t, :], op0=ALU.mult, op1=ALU.mult).then_inc(misc_dve, 1)
                        dve.wait_ge(misc_dve, b * TASKS_BY["dve"] + EMPTIED[key])
                        dve.tensor_tensor(X[:, 4 * g + t, :], X[:, 4 * g + t, :], upd[:, t % 2, :],
                                          ALU.add).then_inc(x_added, 1)
                        dve.wait_ge(x_added, b * 3 * NT + added + 4 * g + t + 1)

            def first_eights(b, n, hh):
                p = n % PAIRS
                dve.wait_ge(row_copied, b * PU_ROWS * PUS + PU_ROWS * n + CHUNKS * (hh + 1))
                apart()
                for i, (qt, base) in enumerate(((p, 0), (NT - 1 - p, (p + 1) * P))):
                    for k, (a, w) in enumerate(segments(qt)):
                        last = dve.max(cand[:, 2 * hh + i, 8 * k:8 * k + 8], score[n % 2][:, hh, base + a:base + a + w])
                return step(last)

            def thresholds(b, n):
                u, p = n // PAIRS, n % PAIRS
                width = [8 * len(segments(qt)) for qt in (p, NT - 1 - p)]
                for h in range(HT):
                    k = step(dve.max(best[:, h, 0:8], cand[:, h, 0:width[h % 2]]))
                settled(b, k)
                apart()
                for h in range(HT):
                    last = step(dve.match_replace(rest[:, h, 0:width[h % 2]], best[:, h, 0:8], cand[:, h, 0:width[h % 2]],
                                                  MASKED))
                settled(b, last)
                apart()
                for h in range(HT):
                    k = step(dve.max(best[:, h, 8:16], rest[:, h, 0:width[h % 2]]))
                for i in range(2):
                    k = step(dve.tensor_reduce(edge[:, :, i], cand[:, i::2, 7:width[i]:8], AX.X, ALU.max))
                settled(b, k)
                k = step(dve.tensor_tensor_scan(cum[:, :, :].rearrange("p h r -> p (h r)"),
                                                carry[:, :, :].rearrange("p h r -> p (h r)"),
                                                best[:, :, :].rearrange("p h r -> p (h r)"), 0.0, ALU.mult, ALU.add))
                edge2 = edge[:, :, :].rearrange("p h a -> p (h a)")
                k2 = step(dve.tensor_tensor(edge2, edge2, best[:, :, TOP - 1], ALU.max))
                settled(b, k2)
                k = step(dve.scalar_tensor_tensor(out=cum[:, :, :], in0=cum[:, :, :], scalar=-1.0, in1=inv_rank[:, :, :],
                                                  op0=ALU.add, op1=ALU.mult))
                settled(b, k)
                if u >= 2:
                    dve.wait_ge(tau_split, b * UNITS + u - 1)
                t = tau[u % 2][:, :, p:NT - p:NT - 1 - 2 * p]
                k = step(dve.tensor_reduce(t, cum[:, :, :].rearrange("p (h a) r -> p h a r", a=2), AX.X, ALU.max))
                settled(b, k)
                k = step(dve.tensor_tensor(flag[:, 0:HT].rearrange("p (h a) -> p h a", a=2), edge[:, :, :], t, ALU.is_gt))
                settled(b, k)
                k = step(dve.tensor_reduce(flag[:, HT:HT + 1], flag[:, 0:HT], AX.X, ALU.max))
                settled(b, k)
                if n >= 2:
                    dve.wait_ge(misc_filled, b * TASKS + TASK[("flag", n - 2)] + 1)
                dve.tensor_copy(flag_b[:, n % 2, :], flag[:, :]).then_inc(flags_ready, 1)

            def settle(b, n):
                u, p = n // PAIRS, n % PAIRS
                key = ("flag", n)
                dve.wait_ge(misc_filled, b * TASKS + TASK[key] + 1)
                dve.tensor_copy(flag_n[:, :], misc_ps[0:1, TASK[key] % 2, 0:HT + 1]).then_inc(misc_dve, 1)
                dve.wait_ge(misc_dve, b * TASKS_BY["dve"] + EMPTIED[key])
                apart()
                flagged = dve.value_load(flag_n[0:1, HT:HT + 1])
                with dve.If(flagged > 0):
                    for i, (qt, base) in enumerate(((p, 0), (NT - 1 - p, (p + 1) * P))):
                        width = (qt + 1) * P
                        with dve.Fori(0, UH) as hh:
                            left = dve.value_load(flag_n[0:1, bass.ds(2 * hh + i, 1)])
                            with dve.If(left > 0):
                                scores = score[n % 2][:, bass.ds(hh, 1), base:base + width].rearrange("p o k -> p (o k)")
                                mine = tau[u % 2][:, bass.ds(hh, 1), qt]
                                newton(scores, mine, width)
                dve.drain().then_inc(pu_settled, 1)

            def newton_steps(scores, width, steps):
                for i in range(steps):
                    dve.scalar_tensor_tensor(out=junk[:, 0:width], in0=scores, scalar=n_tau[:, 0:1], in1=scores,
                                             op0=ALU.is_gt, op1=ALU.mult, accum_out=n_sum[:, :])
                    dve.drain()
                    dve.tensor_scalar(junk[:, 0:width], scores, n_tau[:, 0:1], 0.0, ALU.is_gt, ALU.add,
                                      accum_out=n_cnt[:, i % 2:i % 2 + 1])
                    dve.drain()
                    dve.tensor_scalar(n_inv[:, :], n_cnt[:, i % 2:i % 2 + 1], 1.0, None, ALU.max)
                    dve.drain()
                    dve.reciprocal(n_inv[:, :], n_inv[:, :])
                    dve.drain()
                    dve.tensor_scalar(n_tau[:, :], n_sum[:, :], -1.0, n_inv[:, 0:1], ALU.add, ALU.mult)
                    dve.drain()
                dve.tensor_tensor(n_square[:, 0:1], n_cnt[:, 0:1], n_cnt[:, 1:2], ALU.not_equal)
                dve.drain()
                dve.transpose(n_turned[:, :], n_square[:, :])
                dve.drain()
                dve.tensor_reduce(n_left[:, :], n_turned[:, :], AX.X, ALU.add)
                dve.drain()

            def rows_left():
                return (dve.value_load(n_left[0:1, 0:1]) + dve.value_load(n_left[32:33, 0:1])
                        + dve.value_load(n_left[64:65, 0:1]) + dve.value_load(n_left[96:97, 0:1]))

            def newton(scores, mine, width):
                dve.tensor_copy(n_tau[:, :], mine)
                dve.drain()
                newton_steps(scores, width, 3)
                with dve.If(rows_left() > 0):
                    with dve.Fori(0, ROUNDS):
                        with dve.If(rows_left() > 0):
                            newton_steps(scores, width, 2)
                dve.tensor_copy(mine, n_tau[:, :])
                dve.drain()

            with dve.Fori(0, BATCH) as b:
                chain[0] = 0
                dve.wait_ge(x_loaded, b * 16 + 16)
                ffn(b, 0, 0)
                for g in range(G):
                    normalise(b, 1, g)
                for n in range(T // 256):
                    for w in range(2):
                        for m in range(C):
                            i = 4 * n + 2 * w + m
                            key = ("qk", w, m, n)
                            dve.wait_ge(hi_ready, b * 16 + i + 1)
                            if i >= 2:
                                dve.wait_ge(lo_ready, b * 16 + i - 1)
                            dve.scalar_tensor_tensor(out=res[:, i % 2, :], in0=misc_ps[:, TASK[key] % 2, 0:256],
                                                     scalar=0.25 if w == 0 else 1.0,
                                                     in1=part[w][0][:, m, 256 * n:256 * n + 256],
                                                     op0=ALU.mult, op1=ALU.subtract).then_inc(misc_dve, 1)
                for n in range(PUS):
                    for hh in range(UH):
                        k = first_eights(b, n, hh)
                        if hh == 0 and n:
                            settle(b, n - 1)
                    settled(b, k)
                    apart()
                    thresholds(b, n)
                settle(b, PUS - 1)
                for t in range(NT):
                    key = ("o", t)
                    dve.wait_ge(misc_filled, b * TASKS + TASK[key] + 1)
                    dve.tensor_tensor(X[:, t, :], X[:, t, :], misc_ps[:, TASK[key] % 2, 0:256], ALU.add).then_inc(misc_dve, 1)
                    dve.wait_ge(misc_dve, b * TASKS_BY["dve"] + EMPTIED[key])
                    dve.sem_inc(x_added, 1)
                ffn(b, 1, 2 * NT)
                assert chain[0] == CHAIN, chain[0]


def kernel(**inputs):
    import numpy as _np
    import concourse.bacc as _bacc
    from concourse import mybir as _mybir
    from concourse.bass_utils import run_bass_kernel_spmd as _run

    def rows(w):
        return _np.ascontiguousarray(w.T.reshape(C, P, D).transpose(1, 0, 2))

    def by_feature(w):
        return w.reshape(UNITS, UH, HD, D).transpose(0, 2, 1, 3).reshape(D, D)

    i = {k: _np.asarray(v) for k, v in inputs.items()}
    arrays = {
        "x": i["L0_attn_x"],
        "wr": rows(i["L0_ffn_W_r"]), "wk": rows(i["L0_ffn_W_k"]), "wv": rows(i["L0_ffn_W_v"]),
        "mur": i["L0_ffn_mu_r"].reshape(C, P).T, "muk": i["L0_ffn_mu_k"].reshape(C, P).T,
        "wq": rows(by_feature(i["L0_attn_Wq"])), "wkk": rows(by_feature(i["L0_attn_Wk"])),
        "wvv": rows(i["L0_attn_Wv"]),
        "wo": i["L0_attn_Wo"].T.reshape(UNITS, UH, HD, D).transpose(2, 1, 0, 3),
    }
    arrays = {f"in_{k}": _np.ascontiguousarray(v) for k, v in arrays.items()}
    nc = _bacc.Bacc("TRN2", target_bir_lowering=False, num_devices=1)
    args = [nc.dram_tensor(k, a.shape, _mybir.dt.from_np(a.dtype), kind="ExternalInput").ap()
            for k, a in arrays.items()]
    args.append(nc.dram_tensor("out_dram", (BATCH, T, D), _mybir.dt.float32, kind="ExternalOutput").ap())
    macaron(nc, *args)
    r = _run(nc, [arrays], core_ids=[0])
    return r.results[0]["out_dram"]
```

```python
from contextlib import ExitStack

import concourse.bass as bass
from concourse import mybir

ALU = mybir.AluOpType
ACT = mybir.ActivationFunctionType
AX = mybir.AxisListType
F32 = mybir.dt.float32
BF16 = mybir.dt.bfloat16
I32 = mybir.dt.int32

P = 128
BATCH, T, D, H = 8, 1024, 256, 16
HD = D // H
NT = T // P
C = D // P
UH = 4
UNITS = H // UH
PAIRS = NT // 2
PUS = UNITS * PAIRS
HT = 2 * UH
ROWW = (NT + 1) * P
RUNS = 4
CAND = 8 * RUNS
TOP = 16
MASKED = -1.0e30
EPS = 1e-5
G = 2
TH = T // G
QPART = [0, 0, 1, 1, 0, 2]
KPART = [0, 1, 0, 1, 2, 0]
SROWS = HD * len(QPART)
TROWS = SROWS + 3
ROUNDS = 16


def row_chunks(p):
    out = []
    for qt, base in ((p, 0), (NT - 1 - p, (p + 1) * P)):
        n = (qt + 1) * P
        out += [(qt, a, min(512, n - a), base + a) for a in range(0, n, 512)]
    return out


STEPS = [(s, j, max(TH * s, P * j)) for s in range(G) for j in range(NT * (s + 1) // G)]
STEPS_AT = {4: [0], 5: [1], 6: [2, 3], 7: [4], 8: [5], 9: [6], 10: [7], 11: [8], 12: [9], 13: [10, 11],
            14: [12]}
CHUNKS = 3
PU_ROWS = UH * CHUNKS
UNIT_BLOCKS = UH * len(STEPS)
THR_PU = 10
THR_STEPS = THR_PU * PUS

POSITIONS = PUS * UH


def norm_of(layer, first):
    return [(first, "stats", layer, 0), (first + 1, "root", layer, 0), (first + 2, "scale", layer, 0)]


def unit_of(layer, firsts):
    out = []
    for g, p in enumerate(firsts):
        out += [(p, "norm", layer, g), (p + 1, "turn", layer, g), (p + 3, "mix", layer, g), (p + 4, "gate", layer, g),
                (p + 5, "hidden", layer, g), (p + 8, "value", layer, g)]
    return out


PROJECT = norm_of(1, 42) + [(48, "norm", 1, 0), (49, "turn", 1, 0), (50, "norm", 1, 1), (51, "turn", 1, 1)]
PROJECT += [(50 + i, "qk", i, 1) for i in range(4)] + [(50 + i, "qk", i, 1) for i in range(4, 8)]
AHEAD = norm_of(0, 0) + unit_of(0, (4, 15)) + PROJECT
BEHIND = [(16 + t, "out", t, 2) for t in range(NT // 2)] + norm_of(2, 21) + unit_of(2, (26, 37))
OWN = [(14 + t, "val", t, 1) for t in range(NT // 2)]
AHEAD.sort(key=lambda e: e[0])
BEHIND.sort(key=lambda e: e[0])


def schedule(has_prev, has_next):
    at = [[] for _ in range(POSITIONS + 8)]
    for entries, rel, there in ((BEHIND, -1, has_prev), (OWN, 0, True), (AHEAD, 1, has_next)):
        for p, what, a, b in entries:
            if there:
                at[p].append((what, a, b, rel))
    for u in range(UNITS):
        p, rel = (16 * (u + 1), 0) if u < UNITS - 1 else (0, -1)
        if rel == 0 or has_prev:
            at[p + 1].insert(0, ("split", u, 0, rel))
            at[p + 3].insert(0, ("tau", u, 0, rel))
    return at


def steps_at(pos):
    return pos // 16 - 1, STEPS_AT.get(pos % 16, [])


KINDS = {("yT", 0): 4, ("yT", 1): 4, ("yT", 2): 4, ("gate", 0): 4, ("gate", 2): 4, ("hidden", 0): 4, ("hidden", 2): 4,
         ("value", 0): 4, ("value", 2): 4, "qk": 8, "val": 4, "out": 4, "tau": 4}


BANKS = 7


def first_bank(has_prev, has_next):
    tasks = {"turn": C, "gate": 2, "hidden": C, "value": 2, "qk": 1, "val": 1, "out": 1, "tau": 1}
    used = PU_ROWS * PUS + sum(tasks.get(e[0], 0) for stages in schedule(has_prev, has_next) for e in stages)
    for pos in range(POSITIONS):
        u, steps = steps_at(pos)
        if u >= 0 or has_prev:
            used += UH * sum(k < len(STEPS) for k in steps)
    return -used % BANKS


def counted(value):
    return not isinstance(value, int) or value > 0


def macaron(nc, x_in, wr, wk, wv, mur, muk, wq, wkk, wvv, wo, x1, out):
    with ExitStack() as ctx:
        def sb(name, shape, dt=F32):
            return ctx.enter_context(nc.sbuf_tensor(name, shape, dt))

        def ps(name, shape, dt=F32):
            return ctx.enter_context(nc.psum_tensor(name, shape, dt))

        def sem(name):
            return ctx.enter_context(nc.semaphore(name))

        w_sb = {n: sb("w_" + n, [P, C, D]) for n in ("r", "k", "v", "q", "kk", "vv")}
        wo_sb = sb("wo_sb", [P, UNITS, D])
        mu_sb = sb("mu_sb", [P, 2, C])
        ident = sb("ident", [P, P])
        ident_b = sb("ident_b", [P, P], BF16)
        mask_row = sb("mask_row", [P, P], BF16)
        mask_col = sb("mask_col", [P, P], BF16)
        carry = sb("carry", [P, HT, TOP])
        inv_rank = sb("inv_rank", [P, HT, TOP])
        eps_sb = sb("eps_sb", [P, 1])
        zero_sb = sb("zero_sb", [P, C])

        XA = sb("XA", [P, NT, D])
        XB = sb("XB", [P, NT, D])
        stats = sb("stats", [P, NT, 6])
        mv = sb("mv", [P, NT, 2])
        sd = sb("sd", [P, NT])
        rstd = sb("rstd", [P, NT])
        shift = sb("shift", [P, NT])
        ytok = sb("ytok", [P, 4, D])
        yT = sb("yT", [P, C, TH + 1])
        xr = sb("xr", [P, C, TH])
        xk = sb("xk", [P, C, TH])
        upd = sb("upd", [P, 4, D])
        y2T = sb("y2T", [P, C, T])
        V = sb("V", [P, NT, D])
        part = [[sb(f"part_{w}{i}", [P, C, T], BF16) for i in range(3)] for w in "qk"]
        whole = sb("whole", [P, 2, TH])
        stack = [[sb(f"stack_{w}{i}", [TROWS, UH, T], BF16) for i in range(2)] for w in "qk"]
        OT = sb("OT", [P, UNITS, T])

        score = [sb(f"score{i}", [P, UH, ROWW]) for i in range(2)]
        cand = sb("cand", [P, HT, CAND])
        rest = sb("rest", [P, HT, CAND])
        best = sb("best", [P, HT, TOP])
        cum = sb("cum", [P, HT, TOP])
        edge = sb("edge", [P, UH, 2])
        flag = sb("flag", [P, 2, HT + 1])
        flag_all = sb("flag_all", [P, 2, HT + 1])
        tau = [sb(f"tau{i}", [P, UH, NT]) for i in range(2)]
        ntau = sb("ntau", [P, 2, UH * NT])
        tau_part = sb("tau_part", [P, 3, UH * NT], BF16)
        tauT = sb("tauT", [3 * UH * NT, P], BF16)
        n_tau = sb("n_tau", [P, 1])
        n_sum = sb("n_sum", [P, 1])
        n_cnt = sb("n_cnt", [P, 2])
        n_inv = sb("n_inv", [P, 1])
        n_square = sb("n_square", [P, 32])
        n_turned = sb("n_turned", [P, 32])
        n_left = sb("n_left", [P, 1], I32)
        probs = sb("probs", [P, 2, UH, TH])
        junk = sb("junk", [P, T], BF16)

        bank_ps = ps("bank_ps", [P, BANKS, 512])
        o_ps = ps("o_ps", [P, 512])

        w_loaded, pads_zero, consts = sem("w_loaded"), sem("pads_zero"), sem("consts")
        psum_zeroed, const_chain = sem("psum_zeroed"), sem("const_chain")
        x_loaded, x1_saved, x1_loaded, x_stored = sem("x_loaded"), sem("x1_saved"), sem("x1_loaded"), sem("x_stored")
        by_layer = {}
        for name in ("ln_chain", "stats_ready", "sd_ready", "scale_ready", "y_ready", "diff_ready", "xr_ready",
                     "xk_scaled", "xk_ready", "hidden_ready", "x_added"):
            by_layer[name] = [sem(f"{name}{i}") for i in range(3)]
        ln_chain, stats_ready, sd_ready = by_layer["ln_chain"], by_layer["stats_ready"], by_layer["sd_ready"]
        scale_ready, y_ready, diff_ready = by_layer["scale_ready"], by_layer["y_ready"], by_layer["diff_ready"]
        xr_ready, xk_scaled, xk_ready = by_layer["xr_ready"], by_layer["xk_scaled"], by_layer["xk_ready"]
        hidden_ready, x_added = by_layer["hidden_ready"], by_layer["x_added"]
        filled = {k: sem("filled_" + "".join(map(str, k))) for k in KINDS}
        emptied = {k: sem("emptied_" + "".join(map(str, k))) for k in KINDS}
        rest_ready, lo_ready = sem("rest_ready"), sem("lo_ready")
        gated, out_added = [sem("gated0"), None, sem("gated2")], sem("out_added")
        stack_loaded = [sem("stack_loaded0"), sem("stack_loaded1")]
        unit_scored = sem("unit_scored")
        row_filled, row_copied = sem("row_filled"), sem("row_copied")
        flags_ready, flags_joined, pu_settled = sem("flags_ready"), sem("flags_joined"), sem("pu_settled")
        tau_split, tau_loaded = sem("tau_split"), sem("tau_loaded")
        split_chain = sem("split_chain")
        col_filled, pv_done = sem("col_filled"), sem("pv_done")
        probs_ready = [sem(f"probs_ready{i}") for i in range(UH)]
        o_copied = sem("o_copied")
        thr_chain = sem("thr_chain")
        wait_kept = sem("wait_kept")

        x_v = x_in.rearrange("b (t p) d -> b p t d", p=P)
        out_v = out.rearrange("b (t p) d -> b p t d", p=P)

        ctx.enter_context(nc.allow_low_precision("the operands are split exactly into bfloat16 parts"))
        block = ctx.enter_context(nc.Block())

        def apart(engine):
            engine.sem_inc(wait_kept, 1)

        def batches(engine, before, body, behind):
            before()
            body(0, False, True)
            with engine.Fori(1, BATCH - 1) as b:
                body(b, True, True)
            body(BATCH - 1, True, False)
            behind()

        BEFORE = [e[1:] + (0,) for e in AHEAD]
        BEHIND_LAST = [e[1:] + (BATCH - 1,) for e in BEHIND]

        @block.sync
        def _(sp):
            for t, src in ((w_sb["r"], wr), (w_sb["k"], wk), (w_sb["v"], wv), (w_sb["q"], wq),
                           (w_sb["kk"], wkk), (w_sb["vv"], wvv)):
                sp.dma_start(t[:, :, :], src).then_inc(w_loaded, 16)
            sp.dma_start(mu_sb[:, 0, :], mur).then_inc(w_loaded, 16)
            sp.dma_start(mu_sb[:, 1, :], muk).then_inc(w_loaded, 16)
            sp.wait_ge(pads_zero, 1)
            for h in range(UH):
                sp.dma_start(wo_sb[32 * h:32 * h + HD, :, :], wo[:, h, :, :]).then_inc(w_loaded, 16)

            sp.sem_inc(x_stored, 16)

            def batch_of(dram, b):
                return dram[b] if isinstance(b, int) else dram[bass.ds(b, 1)].rearrange("o p t d -> p (o t) d")

            def scratch(b):
                flat = x1[b] if isinstance(b, int) else x1[bass.ds(b, 1)].rearrange("o p n -> p (o n)")
                return flat.rearrange("p (t d) -> p t d", d=D)

            def load_x(b):
                sp.dma_start(XA[:, :, :], batch_of(x_v, b)).then_inc(x_loaded, 16)

            def save_x1(b):
                sp.wait_ge(x_added[0], b * 4 + 4)
                apart(sp)
                sp.dma_start(scratch(b), XA[:, :, :].rearrange("p t d -> p (t d)").rearrange("p (t d) -> p t d", d=D)
                             ).then_inc(x1_saved, 16)

            def load_stack(b, u):
                sp.wait_ge(lo_ready, b * 8 + 8)
                apart(sp)
                if counted(b * UNITS + u - 1):
                    sp.wait_ge(unit_scored, b * UNITS + u - 1)
                apart(sp)
                rows = slice(64 * (u % 2), 64 * (u % 2) + 64)
                for w, parts in ((0, QPART), (1, KPART)):
                    for j, i in enumerate(parts):
                        sp.dma_start(stack[w][u % 2][HD * j:HD * (j + 1), :, :],
                                     part[w][i][rows, u // 2, :]).then_inc(stack_loaded[u % 2], 16)

            def load_tau(b, u):
                sp.wait_ge(emptied["tau"], b * UNITS + u + 1)
                sp.dma_start(stack[0][u % 2][SROWS:TROWS, :, :], tauT[:, :]).then_inc(tau_loaded, 16)

            def store(b):
                sp.wait_ge(x_added[2], b * 4 + 4)
                apart(sp)
                sp.dma_start(batch_of(out_v, b), XB[:, :, :]).then_inc(x_stored, 16)

            def load_x1(b):
                sp.wait_ge(x_stored, b * 16 + 16)
                apart(sp)
                sp.wait_ge(x1_saved, b * 16 + 16)
                apart(sp)
                sp.dma_start(XB[:, :, :], scratch(b)).then_inc(x1_loaded, 16)

            def body(b, has_prev, has_next):
                at = schedule(has_prev, has_next)
                for pos in range(POSITIONS):
                    if pos == 3 and has_prev:
                        load_x1(b - 1)
                    for what, a, c, rel in at[pos]:
                        if what == "tau":
                            load_tau(b + rel, a)
                    if pos % 16 == 14 and pos < POSITIONS - 16:
                        load_stack(b, pos // 16 + 1)
                    if pos == 26 and has_next:
                        save_x1(b + 1)
                    if pos == 48 and has_prev:
                        store(b - 1)
                    if pos == 51 and has_next and (not isinstance(b, int) or b + 2 < BATCH):
                        sp.wait_ge(x1_saved, b * 16 + 32)
                        apart(sp)
                        sp.wait_ge(y_ready[1], (b + 1) * NT + NT)
                        apart(sp)
                        load_x(b + 2)
                    if pos == 62 and has_next:
                        load_stack(b + 1, 0)

            load_x(0)
            save_x1(0)
            sp.wait_ge(x1_saved, 16)
            sp.wait_ge(y_ready[1], NT)
            load_x(1)
            load_stack(0, 0)
            body(0, False, True)
            with sp.Fori(1, BATCH - 2) as b:
                body(b, True, True)
            body(BATCH - 2, True, True)
            body(BATCH - 1, True, False)
            load_x1(BATCH - 1)
            load_tau(BATCH - 1, UNITS - 1)
            store(BATCH - 1)
            sp.wait_ge(x_stored, BATCH * 16 + 16)

        @block.gpsimd
        def _(pool):
            pool.memset(wo_sb[:, :, :], 0.0).then_inc(pads_zero, 1)
            pool.memset(ident[:, :], 0.0).then_inc(const_chain, 1)
            pool.memset(ident_b[:, :], 0.0).then_inc(const_chain, 1)
            pool.memset(mask_row[:, :], 0.0).then_inc(const_chain, 1)
            pool.memset(mask_col[:, :], 0.0).then_inc(const_chain, 1)
            pool.memset(carry[:, :, :], 1.0).then_inc(const_chain, 1)
            pool.memset(eps_sb[:, :], EPS)
            pool.memset(zero_sb[:, :], 0.0)
            pool.memset(n_square[:, :], 0.0)
            for r in range(TOP):
                pool.memset(inv_rank[:, :, r:r + 1], 1.0 / (r + 1))
            pool.wait_ge(const_chain, 5)
            for t in (ident, ident_b):
                pool.affine_select(out=t[:, :], in_=t[:, :], compare_op=ALU.not_equal, fill=1.0, base=0,
                                   pattern=[[-1, P]], channel_multiplier=1)
            pool.affine_select(out=mask_row[:, :], in_=mask_row[:, :], compare_op=ALU.is_ge, fill=MASKED, base=0,
                               pattern=[[-1, P]], channel_multiplier=1)
            pool.affine_select(out=mask_col[:, :], in_=mask_col[:, :], compare_op=ALU.is_ge, fill=MASKED, base=0,
                               pattern=[[1, P]], channel_multiplier=-1)
            pool.memset(carry[:, :, 0:1], 0.0)
            pool.drain().then_inc(consts, 1)
            pool.wait_ge(w_loaded, 12 * 16)

            def differences(b, layer, g):
                pool.wait_ge(emptied[("yT", layer)], b * 4 + 2 * g + 2)
                for c in range(C):
                    ins = pool.tensor_tensor(xk[:, c, :], yT[:, c, 1:TH + 1], yT[:, c, 0:TH], ALU.subtract)
                ins.then_inc(diff_ready[layer], 1)

            def mix(b, layer, g):
                pool.wait_ge(xr_ready[layer], b * G + g + 1)
                apart(pool)
                for c in range(C):
                    ins = pool.tensor_scalar(xk[:, c, :], xk[:, c, :], mu_sb[:, 1, c:c + 1], 0.0, ALU.mult, ALU.add)
                ins.then_inc(xk_scaled[layer], 1)
                pool.wait_ge(xk_scaled[layer], b * G + g + 1)
                for c in range(C):
                    ins = pool.tensor_tensor(xk[:, c, :], xk[:, c, :], yT[:, c, 0:TH], ALU.add)
                ins.then_inc(xk_ready[layer], 1)

            def square(b, layer, g):
                for m in range(C):
                    pool.wait_ge(emptied[("hidden", layer)], b * 4 + 2 * g + m + 1)
                    ins = pool.tensor_tensor(xr[:, m, :], xr[:, m, :], xr[:, m, :], ALU.mult)
                ins.then_inc(hidden_ready[layer], 1)

            def add_value(b, layer, g):
                X = XA if layer == 0 else XB
                for t in range(2):
                    pool.wait_ge(emptied[("value", layer)], b * 4 + 2 * g + t + 1)
                    two = slice(2 * t, 2 * t + 2)
                    pool.tensor_tensor(upd[:, two, :], upd[:, two, :], ytok[:, two, :], ALU.mult).then_inc(gated[layer], 1)
                for t in range(2):
                    pool.wait_ge(gated[layer], b * 4 + 2 * g + t + 1)
                    at = 4 * g + 2 * t
                    pool.tensor_tensor(X[:, at:at + 2, :], X[:, at:at + 2, :], upd[:, 2 * t:2 * t + 2, :],
                                       ALU.add).then_inc(x_added[layer], 1)

            def add_output(b, t):
                if t == 0:
                    pool.wait_ge(x1_loaded, b * 16 + 16)
                pool.wait_ge(emptied["out"], b * 4 + t + 1)
                at = 2 * (t % 2)
                pool.tensor_tensor(XB[:, 2 * t:2 * t + 2, :], XB[:, 2 * t:2 * t + 2, :], upd[:, at:at + 2, :],
                                   ALU.add).then_inc(out_added, 1)

            def later_parts(b, i):
                g, w, m = i // 4, i // 2 % 2, i % 2
                at = slice(TH * g, TH * (g + 1))
                pool.wait_ge(emptied["qk"], b * 8 + i + 1)
                pool.tensor_tensor(part[w][1][:, m, at], whole[:, i % 2, :], part[w][0][:, m, at], ALU.subtract)
                pool.tensor_tensor(whole[:, i % 2, :], whole[:, i % 2, :], part[w][0][:, m, at],
                                   ALU.subtract).then_inc(rest_ready, 1)
                pool.wait_ge(rest_ready, b * 8 + i + 1)
                pool.tensor_tensor(part[w][2][:, m, at], whole[:, i % 2, :], part[w][1][:, m, at],
                                   ALU.subtract).then_inc(lo_ready, 1)

            def join_flags(b, n):
                pool.wait_ge(flags_ready, b * PUS + n + 1)
                apart(pool)
                pool.partition_all_reduce(flag_all[:, n % 2, :], flag[:, n % 2, :], P,
                                          bass.bass_isa.ReduceOp.max).then_inc(flags_joined, 1)

            def split(b, u):
                pool.wait_ge(pu_settled, b * PUS + PAIRS * (u + 1))
                apart(pool)
                if counted(b * UNITS + u):
                    pool.wait_ge(filled["tau"], b * UNITS + u)
                apart(pool)
                t = tau[u % 2][:, :, :].rearrange("p h q -> p (h q)")
                base = b * UNITS * 5 + 5 * u

                def after(k):
                    pool.wait_ge(split_chain, base + k)
                    apart(pool)

                pool.tensor_scalar(ntau[:, 0, :], t, -1.0, 0.0, ALU.mult, ALU.add).then_inc(split_chain, 1)
                after(1)
                pool.tensor_copy(tau_part[:, 0, :], ntau[:, 0, :]).then_inc(split_chain, 1)
                after(2)
                pool.tensor_tensor(ntau[:, 1, :], ntau[:, 0, :], tau_part[:, 0, :], ALU.subtract).then_inc(split_chain, 1)
                after(3)
                pool.tensor_copy(tau_part[:, 1, :], ntau[:, 1, :]).then_inc(split_chain, 1)
                after(4)
                pool.tensor_tensor(tau_part[:, 2, :], ntau[:, 1, :], tau_part[:, 1, :], ALU.subtract).then_inc(split_chain, 1)
                after(5)
                pool.sem_inc(tau_split, 1)

            def stage(what, a, c, b):
                if what == "turn" and a != 1:
                    differences(b, a, c)
                elif what == "mix":
                    mix(b, a, c)
                elif what == "hidden":
                    square(b, a, c)
                elif what == "value":
                    add_value(b, a, c)
                elif what == "out":
                    add_output(b, a)
                elif what == "qk":
                    later_parts(b, a)
                elif what == "split":
                    split(b, a)

            def before():
                for e in BEFORE:
                    stage(*e)

            def body(b, has_prev, has_next):
                at = schedule(has_prev, has_next)
                for pos in range(POSITIONS):
                    if pos % UH == 0 and pos:
                        join_flags(b, pos // UH - 1)
                    elif pos == 0 and has_prev:
                        join_flags(b - 1, PUS - 1)
                    for what, a, c, rel in at[pos]:
                        stage(what, a, c, b + rel)

            def behind():
                join_flags(BATCH - 1, PUS - 1)
                split(BATCH - 1, UNITS - 1)
                for e in BEHIND_LAST:
                    stage(*e)

            batches(pool, before, body, behind)

        @block.tensor
        def _(pe):
            pe.wait_ge(w_loaded, 12 * 16)
            pe.wait_ge(consts, 1)
            pe.wait_ge(psum_zeroed, 1)
            ring = {"next": 0}
            last_use = {}

            def open_bank(semaphore, per_batch, b, i):
                at = ring["next"]
                if at in last_use:
                    semaphore_then, per_batch_then, b_then, i_then = last_use[at]
                    pe.wait_ge(semaphore_then, b_then * per_batch_then + (i_then + 1))
                last_use[at] = (semaphore, per_batch, b, i)
                ring["next"] = (at + 1) % BANKS
                return bank_ps[:, at, :]

            def open_task(kind, b, i):
                return open_bank(emptied[kind], KINDS[kind], b, i)

            def product(m, left, right):
                for c in range(len(left)):
                    ins = pe.matmul(m, left[c], right[c], start=(c == 0), stop=(c == len(left) - 1))
                return ins

            def turn(b, layer, g):
                kind = ("yT", layer)
                pe.wait_ge(y_ready[layer], b * NT + 4 * g + 4)
                for c in range(C):
                    m = open_task(kind, b, 2 * g + c)
                    for t in range(4):
                        ins = pe.transpose(m[:, P * t:P * (t + 1)], ytok[:, t, P * c:P * (c + 1)], ident[:, :])
                    ins.then_inc(filled[kind], 1)

            def gate(b, layer, g):
                kind = ("gate", layer)
                pe.wait_ge(xr_ready[layer], b * G + g + 1)
                for t in range(2):
                    m = open_task(kind, b, 2 * g + t)
                    for i in range(2):
                        at = P * (2 * t + i)
                        ins = product(m[:, D * i:D * (i + 1)], [xr[:, c, at:at + P] for c in range(C)],
                                      [w_sb["r"][:, c, :] for c in range(C)])
                    ins.then_inc(filled[kind], 1)

            def hidden(b, layer, g):
                kind = ("hidden", layer)
                pe.wait_ge(xk_ready[layer], b * G + g + 1)
                for mm in range(C):
                    m = open_task(kind, b, 2 * g + mm)
                    product(m, [w_sb["k"][:, c, P * mm:P * (mm + 1)] for c in range(C)],
                            [xk[:, c, :] for c in range(C)]).then_inc(filled[kind], 1)

            def value(b, layer, g):
                kind = ("value", layer)
                pe.wait_ge(hidden_ready[layer], b * G + g + 1)
                for t in range(2):
                    m = open_task(kind, b, 2 * g + t)
                    for i in range(2):
                        at = P * (2 * t + i)
                        ins = product(m[:, D * i:D * (i + 1)], [xr[:, c, at:at + P] for c in range(C)],
                                      [w_sb["v"][:, c, :] for c in range(C)])
                    ins.then_inc(filled[kind], 1)

            def project(b, i):
                g, w, mm = i // 4, i // 2 % 2, i % 2
                pe.wait_ge(emptied[("yT", 1)], b * 4 + 2 * g + 2)
                m = open_task("qk", b, i)
                name = ("q", "kk")[w]
                product(m, [w_sb[name][:, c, P * mm:P * (mm + 1)] for c in range(C)],
                        [y2T[:, c, TH * g:TH * (g + 1)] for c in range(C)]).then_inc(filled["qk"], 1)

            def values(b, t):
                m = open_task("val", b, t)
                for i in range(2):
                    at = P * (2 * t + i)
                    ins = product(m[:, D * i:D * (i + 1)], [y2T[:, c, at:at + P] for c in range(C)],
                                  [w_sb["vv"][:, c, :] for c in range(C)])
                ins.then_inc(filled["val"], 1)

            def outputs(b, t):
                pe.wait_ge(o_copied, b * 8 + 8)
                m = open_task("out", b, t)
                for i in range(2):
                    at = P * (2 * t + i)
                    ins = product(m[:, D * i:D * (i + 1)], [OT[:, u, at:at + P] for u in range(UNITS)],
                                  [wo_sb[:, u, :] for u in range(UNITS)])
                ins.then_inc(filled["out"], 1)

            def turn_tau(b, u):
                m = open_task("tau", b, u).bitcast(BF16)
                pe.wait_ge(tau_split, b * UNITS + u + 1)
                pe.transpose(m[0:3 * UH * NT, 0:P], tau_part[:, :, :].rearrange("p a q -> p (a q)"),
                             ident_b[:, :]).then_inc(filled["tau"], 1)

            def scores_head(b, n, hh):
                u, p = n // PAIRS, n % PAIRS
                q, k = stack[0][u % 2], stack[1][u % 2]
                if n % PAIRS == 0 and hh == 0:
                    pe.wait_ge(stack_loaded[u % 2], b * 384 + 192 * (u // 2 + 1))
                for i, (qt, a, w, _) in enumerate(row_chunks(p)):
                    at = PU_ROWS * n + CHUNKS * hh + i
                    bank = open_bank(row_copied, PU_ROWS * PUS, b, at)
                    last = a + w == (qt + 1) * P
                    ins = pe.matmul(bank[:, 0:w], q[0:SROWS, hh, P * qt:P * (qt + 1)], k[0:SROWS, hh, a:a + w],
                                    start=True, stop=not last)
                    if last:
                        ins = pe.matmul(bank[:, w - P:w], ident_b[:, :], mask_row[:, :], start=False, stop=True)
                    ins.then_inc(row_filled, 1)

            def step_scores(b, u, k):
                s, j, q0 = STEPS[k]
                w = TH * (s + 1) - q0
                q, kk = stack[0][u % 2], stack[1][u % 2]
                if k == 0:
                    pe.wait_ge(tau_loaded, b * 64 + 16 * (u + 1))
                diagonal = P * j >= TH * s
                for hh in range(UH):
                    m = open_bank(probs_ready[hh], UNITS * len(STEPS), b, len(STEPS) * u + k)
                    ins = pe.matmul(m[:, 0:w], kk[0:TROWS, hh, P * j:P * (j + 1)], q[0:TROWS, hh, q0:q0 + w],
                                    start=True, stop=not diagonal)
                    if diagonal:
                        ins = pe.matmul(m[:, 0:P], ident_b[:, :], mask_col[:, :], start=False, stop=True)
                    ins.then_inc(col_filled, 1)
                if k == len(STEPS) - 1:
                    pe.wait_ge(col_filled, b * UNITS * UNIT_BLOCKS + UNIT_BLOCKS * (u + 1))
                    pe.sem_inc(unit_scored, 1)

            def step_values(b, u, k):
                s, j, q0 = STEPS[k]
                w = TH * (s + 1) - q0
                if j == 0:
                    if counted(b * 8 + 2 * u + s):
                        pe.wait_ge(o_copied, b * 8 + 2 * u + s)
                    if u == 0 and s == 0:
                        pe.wait_ge(emptied["val"], b * 4 + 4)
                for hh in range(UH):
                    pe.wait_ge(probs_ready[hh], b * UNITS * len(STEPS) + len(STEPS) * u + k + 1)
                    col = (UH * u + hh) * HD
                    ins = pe.matmul(o_ps[32 * hh:32 * hh + HD, TH - w:TH], V[:, j, col:col + HD],
                                    probs[:, k % 2, hh, 0:w], start=(j == 0), stop=(P * (j + 1) == TH * (s + 1)),
                                    skip_group_check=True)
                ins.then_inc(pv_done, 1)

            def second_pass(b, u, steps):
                for k in steps:
                    if k < len(STEPS):
                        step_scores(b, u, k)
                    if k:
                        step_values(b, u, k - 1)

            STAGES = {"turn": turn, "gate": gate, "hidden": hidden, "value": value}

            def stage(what, a, c, b):
                if what in STAGES:
                    STAGES[what](b, a, c)
                elif what == "qk":
                    project(b, a)
                elif what == "val":
                    values(b, a)
                elif what == "out":
                    outputs(b, a)
                elif what == "tau":
                    turn_tau(b, a)

            def before():
                for e in BEFORE:
                    stage(*e)

            def body(b, has_prev, has_next):
                ring["next"] = first_bank(has_prev, has_next)
                if has_prev:
                    for at, (semaphore, per_batch, _, i) in last_use.items():
                        last_use[at] = (semaphore, per_batch, b, i - per_batch)
                at = schedule(has_prev, has_next)
                for pos in range(POSITIONS):
                    n, hh = divmod(pos, UH)
                    scores_head(b, n, hh)
                    for what, a, c, rel in at[pos]:
                        stage(what, a, c, b + rel)
                    u, steps = steps_at(pos)
                    if u >= 0 or has_prev:
                        second_pass(b if u >= 0 else b - 1, u % UNITS, steps)

            def behind():
                b = BATCH - 1
                turn_tau(b, UNITS - 1)
                second_pass(b, UNITS - 1, range(len(STEPS) + 1))
                for e in BEHIND_LAST:
                    stage(*e)

            batches(pe, before, body, behind)

        @block.scalar
        def _(act):
            act.wait_ge(consts, 1)
            ring = {"next": 0}

            def root(b, layer):
                act.wait_ge(stats_ready[layer], b + 1)
                act.activation(sd[:, :], mv[:, :, 1], ACT.Sqrt, bias=eps_sb[:, 0:1]).then_inc(sd_ready[layer], 1)

            def normalise(b, layer, g):
                X = XB if layer == 2 else XA
                act.wait_ge(scale_ready[layer], b + 1)
                if layer == 0 and g == 1:
                    act.wait_ge(gated[0], b * 4 + 2)
                elif layer == 1 and g == 0 and counted(b):
                    act.wait_ge(gated[2], b * 4 - 4)
                elif layer == 2 and g == 0:
                    act.wait_ge(gated[0], last_unit(b) * 4 + 4)
                elif layer == 2:
                    act.wait_ge(gated[2], b * 4 + 2)
                for t in range(4):
                    at = 4 * g + t
                    act.activation(ytok[:, t, :], X[:, at, :], ACT.Identity, bias=shift[:, at:at + 1],
                                   scale=rstd[:, at:at + 1]).then_inc(y_ready[layer], 1)

            def last_unit(b):
                return min(b + 2, BATCH - 1) if isinstance(b, int) else b + 2

            def turned(b, layer, g):
                kind = ("yT", layer)
                for c in range(C):
                    act.wait_ge(filled[kind], b * 4 + 2 * g + c + 1)
                    m = bank_ps[:, bank(), :]
                    if layer == 1:
                        act.activation(y2T[:, c, TH * g:TH * (g + 1)], m, ACT.Copy).then_inc(emptied[kind], 1)
                        continue
                    if c == 0:
                        act.activation(yT[:, :, 0], zero_sb[:, :] if g == 0 else yT[:, :, TH], ACT.Copy)
                        act.drain()
                    act.activation(yT[:, c, 1:TH + 1], m, ACT.Copy).then_inc(emptied[kind], 1)

            def two_tiles(t):
                return bank_ps[:, bank(), :].rearrange("p (t d) -> p t d", d=D), slice(2 * t, 2 * t + 2)

            def gates(b, layer, g):
                kind = ("gate", layer)
                for t in range(2):
                    act.wait_ge(filled[kind], b * 4 + 2 * g + t + 1)
                    m, two = two_tiles(t)
                    act.activation(ytok[:, two, :], m, ACT.Sigmoid).then_inc(emptied[kind], 1)

            def hidden(b, layer, g):
                kind = ("hidden", layer)
                for mm in range(C):
                    act.wait_ge(filled[kind], b * 4 + 2 * g + mm + 1)
                    act.activation(xr[:, mm, :], bank_ps[:, bank(), :], ACT.Relu).then_inc(emptied[kind], 1)

            def value(b, layer, g):
                kind = ("value", layer)
                if layer == 0 and g == 0 and counted(b - 1):
                    act.wait_ge(x_stored, b * 16 - 16)
                elif layer == 0 and g == 1:
                    act.wait_ge(x_added[0], b * 4 + 2)
                    if counted(b - 1):
                        act.wait_ge(out_added, b * 4 - 4)
                elif layer == 2 and g == 0:
                    act.wait_ge(x_added[0], last_unit(b) * 4 + 4)
                elif layer == 2:
                    act.wait_ge(x_added[2], b * 4 + 2)
                for t in range(2):
                    act.wait_ge(filled[kind], b * 4 + 2 * g + t + 1)
                    m, two = two_tiles(t)
                    act.activation(upd[:, two, :], m, ACT.Copy, scale=0.5).then_inc(emptied[kind], 1)

            def output(b, t):
                if t == 0:
                    act.wait_ge(x1_loaded, b * 16 + 16)
                    act.wait_ge(x_added[0], last_unit(b) * 4 + 2)
                elif t >= 2:
                    act.wait_ge(out_added, b * 4 + t - 1)
                act.wait_ge(filled["out"], b * 4 + t + 1)
                m, two = two_tiles(t % 2)
                act.activation(upd[:, two, :], m, ACT.Copy).then_inc(emptied["out"], 1)

            def parts(b, i):
                g, w, m = i // 4, i // 2 % 2, i % 2
                if i == 0 and counted(b):
                    act.wait_ge(stack_loaded[1], b * 384)
                if counted(b * 8 + i - 1):
                    act.wait_ge(lo_ready, b * 8 + i - 1)
                act.wait_ge(filled["qk"], b * 8 + i + 1)
                scale, bk = (0.25 if w == 0 else 1.0), bank()
                act.activation(whole[:, i % 2, :], bank_ps[:, bk, :], ACT.Copy, scale=scale)
                act.activation(part[w][0][:, m, TH * g:TH * (g + 1)], bank_ps[:, bk, :], ACT.Copy,
                               scale=scale).then_inc(emptied["qk"], 1)

            def values(b, t):
                act.wait_ge(filled["val"], b * 4 + t + 1)
                m, two = two_tiles(t)
                act.activation(V[:, two, :], m, ACT.Copy).then_inc(emptied["val"], 1)

            def turned_tau(b, u):
                act.wait_ge(filled["tau"], b * UNITS + u + 1)
                if counted(b * 64 + 16 * u):
                    act.wait_ge(tau_loaded, b * 64 + 16 * u)
                act.activation(tauT[:, :], bank_ps[:, bank(), :].bitcast(BF16)[0:3 * UH * NT, 0:P],
                               ACT.Copy).then_inc(emptied["tau"], 1)

            def copy_head(b, n, hh):
                if hh == 0:
                    if counted(b * PUS + n - 1):
                        act.wait_ge(pu_settled, b * PUS + n - 1)
                for i, (qt, a, w, place) in enumerate(row_chunks(n % PAIRS)):
                    at = PU_ROWS * n + CHUNKS * hh + i
                    act.wait_ge(row_filled, b * PU_ROWS * PUS + at + 1)
                    act.activation(score[n % 2][:, hh, place:place + w], bank_ps[:, bank(), 0:w],
                                   ACT.Copy).then_inc(row_copied, 1)

            def step_probs(b, u, k):
                s, j, q0 = STEPS[k]
                w = TH * (s + 1) - q0
                if counted(b * 48 + 12 * u + k - 1):
                    act.wait_ge(pv_done, b * 48 + 12 * u + k - 1)
                for hh in range(UH):
                    at = UNIT_BLOCKS * u + UH * k + hh
                    act.wait_ge(col_filled, b * UNITS * UNIT_BLOCKS + at + 1)
                    act.activation(probs[:, k % 2, hh, 0:w], bank_ps[:, bank(), 0:w], ACT.Relu).then_inc(probs_ready[hh], 1)

            def output_half(b, u, s):
                act.wait_ge(pv_done, b * 48 + 12 * u + (4 if s == 0 else 12))
                if u == 0 and s == 0:
                    if counted(b * 8):
                        act.wait_ge(filled["out"], b * 4)
                act.activation(OT[:, u, TH * s:TH * (s + 1)], o_ps[:, :], ACT.Copy).then_inc(o_copied, 1)

            def second_pass(b, u, steps):
                for k in steps:
                    if k < len(STEPS):
                        step_probs(b, u, k)
                    if k == 4:
                        output_half(b, u, 0)
                    if k == len(STEPS):
                        output_half(b, u, 1)

            def bank():
                at = ring["next"]
                ring["next"] = (at + 1) % BANKS
                return at

            def stage(what, a, c, b):
                if what == "root":
                    root(b, a)
                elif what == "norm":
                    normalise(b, a, c)
                elif what == "turn":
                    turned(b, a, c)
                elif what == "gate":
                    gates(b, a, c)
                elif what == "hidden":
                    hidden(b, a, c)
                elif what == "value":
                    value(b, a, c)
                elif what == "qk":
                    parts(b, a)
                elif what == "val":
                    values(b, a)
                elif what == "out":
                    output(b, a)
                elif what == "tau":
                    turned_tau(b, a)

            def before():
                for e in BEFORE:
                    stage(*e)

            def body(b, has_prev, has_next):
                ring["next"] = first_bank(has_prev, has_next)
                at = schedule(has_prev, has_next)
                for pos in range(POSITIONS):
                    n, hh = divmod(pos, UH)
                    copy_head(b, n, hh)
                    for what, a, c, rel in at[pos]:
                        stage(what, a, c, b + rel)
                    u, steps = steps_at(pos)
                    if u >= 0 or has_prev:
                        second_pass(b if u >= 0 else b - 1, u % UNITS, steps)

            def behind():
                b = BATCH - 1
                turned_tau(b, UNITS - 1)
                second_pass(b, UNITS - 1, range(len(STEPS) + 1))
                for e in BEHIND_LAST:
                    stage(*e)

            batches(act, before, body, behind)

        @block.vector
        def _(dve):
            for i in range(2):
                dve.memset(stack[1][i][SROWS:TROWS, :, :], 1.0)
            dve.memset(o_ps[:, :], 0.0).then_inc(psum_zeroed, 1)
            dve.wait_ge(consts, 1)
            dve.wait_ge(w_loaded, 12 * 16)

            def statistics(b, layer):
                X = XB if layer == 2 else XA
                if layer == 0:
                    dve.wait_ge(x_loaded, b * 16 + 16)
                elif layer == 1:
                    dve.wait_ge(x_added[0], b * 4 + 4)
                else:
                    dve.wait_ge(out_added, b * 4 + 4)
                for t in range(NT):
                    ins = dve.bn_stats(stats[:, t, :], X[:, t, :])
                ins.then_inc(ln_chain[layer], 1)
                dve.wait_ge(ln_chain[layer], b * 3 + 1)
                apart(dve)
                for t in range(NT):
                    ins = dve.bn_aggr(mv[:, t, :], stats[:, t, :])
                ins.then_inc(stats_ready[layer], 1)

            def scale(b, layer):
                dve.wait_ge(sd_ready[layer], b + 1)
                dve.reciprocal(rstd[:, :], sd[:, :]).then_inc(ln_chain[layer], 1)
                dve.wait_ge(ln_chain[layer], b * 3 + 2)
                dve.scalar_tensor_tensor(out=shift[:, :], in0=mv[:, :, 0], scalar=-1.0, in1=rstd[:, :], op0=ALU.mult,
                                         op1=ALU.mult).then_inc(ln_chain[layer], 1)
                dve.wait_ge(ln_chain[layer], b * 3 + 3)
                dve.sem_inc(scale_ready[layer], 1)

            def mix(b, layer, g):
                dve.wait_ge(diff_ready[layer], b * G + g + 1)
                for c in range(C):
                    ins = dve.scalar_tensor_tensor(out=xr[:, c, :], in0=xk[:, c, :], scalar=mu_sb[:, 0, c:c + 1],
                                                   in1=yT[:, c, 0:TH], op0=ALU.mult, op1=ALU.add)
                ins.then_inc(xr_ready[layer], 1)

            def first_eights(b, n, hh):
                p = n % PAIRS
                dve.wait_ge(row_copied, b * PU_ROWS * PUS + PU_ROWS * n + CHUNKS * (hh + 1))
                apart(dve)
                for i, (qt, base) in enumerate(((p, 0), (NT - 1 - p, (p + 1) * P))):
                    for k in range(RUNS):
                        last = dve.max(cand[:, 2 * hh + i, 8 * k:8 * k + 8],
                                       score[n % 2][:, hh, base + k:base + (qt + 1) * P:RUNS])
                return last

            def thresholds(b, n, last):
                u, p = n // PAIRS, n % PAIRS
                count = [b * THR_STEPS + THR_PU * n]
                done = [0]

                def link(ins):
                    done[0] += 1
                    ins.then_inc(thr_chain, 1)

                def after(back=0):
                    dve.wait_ge(thr_chain, count[0] + done[0] - back)

                edge2 = edge[:, :, :].rearrange("p h a -> p (h a)")
                link(last)
                after()
                apart(dve)
                for h in range(HT):
                    last = dve.max(best[:, h, 0:8], cand[:, h, :])
                link(last)
                link(dve.tensor_reduce(edge2, cand[:, :, 7:CAND:8], AX.X, ALU.max))
                after(1)
                apart(dve)
                for h in range(HT):
                    last = dve.match_replace(rest[:, h, :], best[:, h, 0:8], cand[:, h, :], MASKED)
                link(last)
                after()
                apart(dve)
                for h in range(HT):
                    last = dve.max(best[:, h, 8:16], rest[:, h, :])
                link(last)
                after()
                link(dve.tensor_tensor_scan(cum[:, :, :].rearrange("p h r -> p (h r)"),
                                            carry[:, :, :].rearrange("p h r -> p (h r)"),
                                            best[:, :, :].rearrange("p h r -> p (h r)"), 0.0, ALU.mult, ALU.add))
                link(dve.tensor_tensor(edge2, edge2, best[:, :, TOP - 1], ALU.max))
                after(1)
                link(dve.scalar_tensor_tensor(out=cum[:, :, :], in0=cum[:, :, :], scalar=-1.0, in1=inv_rank[:, :, :],
                                              op0=ALU.add, op1=ALU.mult))
                if counted(b * UNITS + u - 1):
                    dve.wait_ge(tau_split, b * UNITS + u - 1)
                after()
                t = tau[u % 2][:, :, p:NT - p:NT - 1 - 2 * p]
                link(dve.tensor_reduce(t, cum[:, :, :].rearrange("p (h a) r -> p h a r", a=2), AX.X, ALU.max))
                after()
                mine = flag[:, n % 2, :]
                link(dve.tensor_tensor(mine[:, 0:HT].rearrange("p (h a) -> p h a", a=2), edge[:, :, :], t, ALU.is_gt))
                after()
                dve.tensor_reduce(mine[:, HT:HT + 1], mine[:, 0:HT], AX.X, ALU.max).then_inc(flags_ready, 1)
                assert done[0] == THR_PU, done[0]

            def settle(b, n):
                u, p = n // PAIRS, n % PAIRS
                dve.wait_ge(flags_joined, b * PUS + n + 1)
                apart(dve)
                joined = flag_all[0:1, n % 2, :].bitcast(I32)
                flagged = dve.value_load(joined[:, HT:HT + 1])
                with dve.If(flagged > 0):
                    for i, (qt, base) in enumerate(((p, 0), (NT - 1 - p, (p + 1) * P))):
                        width = (qt + 1) * P
                        with dve.Fori(0, UH) as hh:
                            left = dve.value_load(joined[:, bass.ds(2 * hh + i, 1)])
                            with dve.If(left > 0):
                                scores = score[n % 2][:, bass.ds(hh, 1), base:base + width].rearrange("p o k -> p (o k)")
                                newton(scores, tau[u % 2][:, bass.ds(hh, 1), qt], width)
                dve.drain().then_inc(pu_settled, 1)

            def newton_steps(scores, width, steps):
                for i in range(steps):
                    dve.scalar_tensor_tensor(out=junk[:, 0:width], in0=scores, scalar=n_tau[:, 0:1], in1=scores,
                                             op0=ALU.is_gt, op1=ALU.mult, accum_out=n_sum[:, :])
                    dve.drain()
                    dve.tensor_scalar(junk[:, 0:width], scores, n_tau[:, 0:1], 0.0, ALU.is_gt, ALU.add,
                                      accum_out=n_cnt[:, i % 2:i % 2 + 1])
                    dve.drain()
                    dve.tensor_scalar(n_inv[:, :], n_cnt[:, i % 2:i % 2 + 1], 1.0, None, ALU.max)
                    dve.drain()
                    dve.reciprocal(n_inv[:, :], n_inv[:, :])
                    dve.drain()
                    dve.tensor_scalar(n_tau[:, :], n_sum[:, :], -1.0, n_inv[:, 0:1], ALU.add, ALU.mult)
                    dve.drain()
                dve.tensor_tensor(n_square[:, 0:1], n_cnt[:, 0:1], n_cnt[:, 1:2], ALU.not_equal)
                dve.drain()
                dve.transpose(n_turned[:, :], n_square[:, :])
                dve.drain()
                dve.tensor_reduce(n_left[:, :], n_turned[:, :], AX.X, ALU.add)
                dve.drain()

            def rows_left():
                return (dve.value_load(n_left[0:1, 0:1]) + dve.value_load(n_left[32:33, 0:1])
                        + dve.value_load(n_left[64:65, 0:1]) + dve.value_load(n_left[96:97, 0:1]))

            def newton(scores, mine, width):
                dve.tensor_copy(n_tau[:, :], mine)
                dve.drain()
                newton_steps(scores, width, 3)
                with dve.If(rows_left() > 0):
                    with dve.Fori(0, ROUNDS):
                        with dve.If(rows_left() > 0):
                            newton_steps(scores, width, 2)
                dve.tensor_copy(mine, n_tau[:, :])
                dve.drain()

            def stage(what, a, c, b):
                if what == "stats":
                    statistics(b, a)
                elif what == "scale":
                    scale(b, a)
                elif what == "mix":
                    mix(b, a, c)

            def before():
                for e in BEFORE:
                    stage(*e)

            def body(b, has_prev, has_next):
                at = schedule(has_prev, has_next)
                for pos in range(POSITIONS):
                    n, hh = divmod(pos, UH)
                    last = first_eights(b, n, hh)
                    if hh == 1 and n:
                        settle(b, n - 1)
                    elif hh == 1 and has_prev:
                        settle(b - 1, PUS - 1)
                    for what, a, c, rel in at[pos]:
                        stage(what, a, c, b + rel)
                    if hh == UH - 1:
                        thresholds(b, n, last)

            def behind():
                settle(BATCH - 1, PUS - 1)
                for e in BEHIND_LAST:
                    stage(*e)

            batches(dve, before, body, behind)


def kernel(**inputs):
    import numpy as _np
    import concourse.bacc as _bacc
    from concourse import mybir as _mybir
    from concourse.bass_utils import run_bass_kernel_spmd as _run

    def rows(w):
        return _np.ascontiguousarray(w.T.reshape(C, P, D).transpose(1, 0, 2))

    def by_feature(w):
        return w.reshape(UNITS, UH, HD, D).transpose(0, 2, 1, 3).reshape(D, D)

    i = {k: _np.asarray(v) for k, v in inputs.items()}
    arrays = {
        "x": i["L0_attn_x"],
        "wr": rows(i["L0_ffn_W_r"]), "wk": rows(i["L0_ffn_W_k"]), "wv": rows(i["L0_ffn_W_v"]),
        "mur": i["L0_ffn_mu_r"].reshape(C, P).T, "muk": i["L0_ffn_mu_k"].reshape(C, P).T,
        "wq": rows(by_feature(i["L0_attn_Wq"])), "wkk": rows(by_feature(i["L0_attn_Wk"])),
        "wvv": rows(i["L0_attn_Wv"]),
        "wo": i["L0_attn_Wo"].T.reshape(UNITS, UH, HD, D).transpose(2, 1, 0, 3),
    }
    arrays = {f"in_{k}": _np.ascontiguousarray(v) for k, v in arrays.items()}
    nc = _bacc.Bacc("TRN2", target_bir_lowering=False, num_devices=1)
    args = [nc.dram_tensor(k, a.shape, _mybir.dt.from_np(a.dtype), kind="ExternalInput").ap()
            for k, a in arrays.items()]
    args.append(nc.dram_tensor("x1_scratch", (BATCH, P, NT * D), _mybir.dt.float32, kind="Internal").ap())
    args.append(nc.dram_tensor("out_dram", (BATCH, T, D), _mybir.dt.float32, kind="ExternalOutput").ap())
    macaron(nc, *args)
    r = _run(nc, [arrays], core_ids=[0])
    return r.results[0]["out_dram"]
```

```python
from contextlib import ExitStack

import concourse.bass as bass
from concourse import mybir

ALU = mybir.AluOpType
ACT = mybir.ActivationFunctionType
AX = mybir.AxisListType
F32 = mybir.dt.float32
BF16 = mybir.dt.bfloat16
I32 = mybir.dt.int32

P = 128
BATCH, T, D, H = 8, 1024, 256, 16
HD = D // H
NT = T // P
C = D // P
UH = 4
UNITS = H // UH
PAIRS = NT // 2
PUS = UNITS * PAIRS
HT = 2 * UH
ROWW = (NT + 1) * P
RUNS = 4
CAND = 8 * RUNS
TOP = 16
MASKED = -1.0e30
EPS = 1e-5
G = 2
TH = T // G
QPART = [0, 0, 1, 1, 0, 2]
KPART = [0, 1, 0, 1, 2, 0]
SROWS = HD * len(QPART)
TROWS = SROWS + 3
ROUNDS = 16


def row_chunks(p):
    out = []
    for qt, base in ((p, 0), (NT - 1 - p, (p + 1) * P)):
        n = (qt + 1) * P
        out += [(qt, a, min(512, n - a), base + a) for a in range(0, n, 512)]
    return out


STEPS = [(s, j, max(TH * s, P * j)) for s in range(G) for j in range(NT * (s + 1) // G)]
STEPS_AT = {4: [0], 5: [1, 2], 6: [3, 4], 7: [5], 8: [6], 9: [7], 10: [8], 11: [9], 12: [10, 11],
            13: [12]}
CHUNKS = 3
PU_ROWS = UH * CHUNKS
UNIT_BLOCKS = UH * len(STEPS)
THR_PU = 10
THR_STEPS = THR_PU * PUS

POSITIONS = PUS * UH


def norm_of(layer, first, turns):
    out = [(first, "stats", layer, 0), (first + 4, "root", layer, 0), (first + 4, "scale", layer, 0)]
    for g, p in enumerate(turns):
        out += [(p - 1, "norm", layer, g), (p, "turn", layer, 2 * g), (p + 1, "turn", layer, 2 * g + 1)]
    return out


def unit_of(layer, turns):
    out = []
    for g, p in enumerate(turns):
        out += [(p + 1, "mix", layer, g)]
        for i in range(2):
            out += [(p + 5, "gate", layer, 2 * g + i), (p + 7, "hidden", layer, 2 * g + i),
                    (p + 9 + i, "value", layer, 2 * g + i)]
    return out


AHEAD = norm_of(0, 0, (9, 21)) + unit_of(0, (9, 21))
AHEAD += norm_of(1, 33, (40, 46)) + [(49 + i, "qk", i, 1) for i in range(8)]
BEHIND = [(20 + t, "out", t, 2) for t in range(NT // 2)] + norm_of(2, 24, (33, 43)) + unit_of(2, (33, 43))
OWN = [(15 + (t + 1) // 2, "val", t, 1) for t in range(NT // 2)]
AHEAD.sort(key=lambda e: e[0])
BEHIND.sort(key=lambda e: e[0])


def schedule(has_prev, has_next):
    at = [[] for _ in range(POSITIONS + 8)]
    for entries, rel, there in ((BEHIND, -1, has_prev), (OWN, 0, True), (AHEAD, 1, has_next)):
        for p, what, a, b in entries:
            if there:
                at[p].append((what, a, b, rel))
    for u in range(UNITS):
        p, rel = (16 * (u + 1), 0) if u < UNITS - 1 else (0, -1)
        if rel == 0 or has_prev:
            at[p].insert(0, ("split", u, 0, rel))
            at[p + 3].insert(0, ("tau", u, 0, rel))
    return at


def steps_at(pos):
    return pos // 16 - 1, STEPS_AT.get(pos % 16, [])


def settle_at(n):
    return 0 if n % PAIRS == 0 else 1


KINDS = {("yT", 0): 4, ("yT", 1): 4, ("yT", 2): 4, ("gate", 0): 4, ("gate", 2): 4, ("hidden", 0): 4, ("hidden", 2): 4,
         ("value", 0): 4, ("value", 2): 4, "qk": 8, "val": 4, "out": 4, "tau": 4}


BANKS = 7


def first_bank(has_prev, has_next):
    tasks = ("turn", "gate", "hidden", "value", "qk", "val", "out", "tau")
    used = PU_ROWS * PUS + sum(e[0] in tasks for stages in schedule(has_prev, has_next) for e in stages)
    for pos in range(POSITIONS):
        u, steps = steps_at(pos)
        if u >= 0 or has_prev:
            used += UH * sum(k < len(STEPS) for k in steps)
    return -used % BANKS


def counted(value):
    return not isinstance(value, int) or value > 0


def macaron(nc, x_in, wr, wk, wv, mur, muk, wq, wkk, wvv, wo, x1, out):
    with ExitStack() as ctx:
        def sb(name, shape, dt=F32):
            return ctx.enter_context(nc.sbuf_tensor(name, shape, dt))

        def ps(name, shape, dt=F32):
            return ctx.enter_context(nc.psum_tensor(name, shape, dt))

        def sem(name):
            return ctx.enter_context(nc.semaphore(name))

        w_sb = {n: sb("w_" + n, [P, C, D]) for n in ("r", "k", "v", "q", "kk", "vv")}
        wo_sb = sb("wo_sb", [P, UNITS, D])
        mu_sb = sb("mu_sb", [P, 2, C])
        ident = sb("ident", [P, P])
        ident_b = sb("ident_b", [P, P], BF16)
        mask_row = sb("mask_row", [P, P], BF16)
        mask_col = sb("mask_col", [P, P], BF16)
        carry = sb("carry", [P, HT, TOP])
        inv_rank = sb("inv_rank", [P, HT, TOP])
        eps_sb = sb("eps_sb", [P, 1])
        zero_sb = sb("zero_sb", [P, C])

        XA = sb("XA", [P, NT, D])
        XB = sb("XB", [P, NT, D])
        stats = sb("stats", [P, NT, 6])
        mv = [sb(f"mv{i}", [P, NT, 2]) for i in range(3)]
        sd = [sb(f"sd{i}", [P, NT]) for i in range(3)]
        rstd = [sb(f"rstd{i}", [P, NT]) for i in range(3)]
        shift = [sb(f"shift{i}", [P, NT]) for i in range(3)]
        ytok = sb("ytok", [P, 4, D])
        yT = sb("yT", [P, C, TH + 1])
        xr = sb("xr", [P, C, TH])
        xk = sb("xk", [P, C, TH])
        upd = sb("upd", [P, 4, D])
        y2T = sb("y2T", [P, C, T])
        V = sb("V", [P, NT, D])
        part = [[sb(f"part_{w}{i}", [P, C, T], BF16) for i in range(3)] for w in "qk"]
        whole = sb("whole", [P, 2, TH])
        stack = [[sb(f"stack_{w}{i}", [TROWS, UH, T], BF16) for i in range(2)] for w in "qk"]
        OT = sb("OT", [P, UNITS, T])

        score = [sb(f"score{i}", [P, UH, ROWW]) for i in range(2)]
        cand = sb("cand", [P, HT, CAND])
        rest = sb("rest", [P, HT, CAND])
        best = sb("best", [P, HT, TOP])
        cum = sb("cum", [P, HT, TOP])
        edge = sb("edge", [P, UH, 2])
        flag = sb("flag", [P, 2, HT + 1])
        flag_all = sb("flag_all", [P, 2, HT + 1])
        tau = [sb(f"tau{i}", [P, UH, NT]) for i in range(2)]
        ntau = sb("ntau", [P, 2, UH * NT])
        tau_part = sb("tau_part", [P, 3, UH * NT], BF16)
        tauT = sb("tauT", [3 * UH * NT, P], BF16)
        n_tau = sb("n_tau", [P, 1])
        n_sum = sb("n_sum", [P, 1])
        n_cnt = sb("n_cnt", [P, 2])
        n_inv = sb("n_inv", [P, 1])
        n_square = sb("n_square", [P, 32])
        n_turned = sb("n_turned", [P, 32])
        n_left = sb("n_left", [P, 1], I32)
        probs = sb("probs", [P, 2, UH, TH])
        junk = sb("junk", [P, T], BF16)

        bank_ps = ps("bank_ps", [P, BANKS, 512])
        o_ps = ps("o_ps", [P, 512])

        w_loaded, pads_zero, consts = sem("w_loaded"), sem("pads_zero"), sem("consts")
        psum_zeroed, const_chain = sem("psum_zeroed"), sem("const_chain")
        x_loaded, x1_saved, x1_loaded, x_stored = sem("x_loaded"), sem("x1_saved"), sem("x1_loaded"), sem("x_stored")
        by_layer = {}
        for name in ("ln_chain", "stats_ready", "sd_ready", "scale_ready", "y_ready", "mix_chain", "xr_ready",
                     "xk_ready", "hidden_ready", "x_added"):
            by_layer[name] = [sem(f"{name}{i}") for i in range(3)]
        ln_chain, stats_ready, sd_ready = by_layer["ln_chain"], by_layer["stats_ready"], by_layer["sd_ready"]
        scale_ready, y_ready, mix_chain = by_layer["scale_ready"], by_layer["y_ready"], by_layer["mix_chain"]
        xr_ready, xk_ready = by_layer["xr_ready"], by_layer["xk_ready"]
        hidden_ready, x_added = by_layer["hidden_ready"], by_layer["x_added"]
        filled = {k: sem("filled_" + "".join(map(str, k))) for k in KINDS}
        emptied = {k: sem("emptied_" + "".join(map(str, k))) for k in KINDS}
        rest_ready, lo_ready = sem("rest_ready"), sem("lo_ready")
        gated, out_added = [sem("gated0"), None, sem("gated2")], sem("out_added")
        stack_loaded = [sem("stack_loaded0"), sem("stack_loaded1")]
        unit_scored = sem("unit_scored")
        row_filled, row_copied = sem("row_filled"), sem("row_copied")
        flags_ready, flags_joined, pu_settled = sem("flags_ready"), sem("flags_joined"), sem("pu_settled")
        tau_split, tau_loaded = sem("tau_split"), sem("tau_loaded")
        split_chain = sem("split_chain")
        col_filled, pv_done = sem("col_filled"), sem("pv_done")
        probs_ready = [sem(f"probs_ready{i}") for i in range(UH)]
        o_copied = sem("o_copied")
        thr_chain = sem("thr_chain")
        wait_kept = sem("wait_kept")

        x_v = x_in.rearrange("b (t p) d -> b p t d", p=P)
        out_v = out.rearrange("b (t p) d -> b p t d", p=P)

        ctx.enter_context(nc.allow_low_precision("the operands are split exactly into bfloat16 parts"))
        block = ctx.enter_context(nc.Block())

        def apart(engine):
            engine.sem_inc(wait_kept, 1)

        def batches(engine, before, body, behind):
            before()
            body(0, False, True)
            with engine.Fori(1, BATCH - 1) as b:
                body(b, True, True)
            body(BATCH - 1, True, False)
            behind()

        BEFORE = [e[1:] + (0,) for e in AHEAD]
        BEHIND_LAST = [e[1:] + (BATCH - 1,) for e in BEHIND]

        def token_work(e):
            def mix(b, layer, g):
                for c in range(C):
                    e.wait_ge(emptied[("yT", layer)], b * 4 + 2 * g + c + 1)
                    ins = e.tensor_tensor(xk[:, c, :], yT[:, c, 1:TH + 1], yT[:, c, 0:TH], ALU.subtract)
                ins.then_inc(mix_chain[layer], 1)
                e.wait_ge(mix_chain[layer], b * 6 + 3 * g + 1)
                apart(e)
                for c in range(C):
                    ins = e.tensor_scalar(xr[:, c, :], xk[:, c, :], mu_sb[:, 0, c:c + 1], 0.0, ALU.mult, ALU.add)
                ins.then_inc(mix_chain[layer], 1)
                e.wait_ge(mix_chain[layer], b * 6 + 3 * g + 2)
                for c in range(C):
                    ins = e.tensor_tensor(xr[:, c, :], xr[:, c, :], yT[:, c, 0:TH], ALU.add)
                ins.then_inc(xr_ready[layer], 1)
                for c in range(C):
                    ins = e.tensor_scalar(xk[:, c, :], xk[:, c, :], mu_sb[:, 1, c:c + 1], 0.0, ALU.mult, ALU.add)
                ins.then_inc(mix_chain[layer], 1)
                e.wait_ge(mix_chain[layer], b * 6 + 3 * g + 3)
                for c in range(C):
                    ins = e.tensor_tensor(xk[:, c, :], xk[:, c, :], yT[:, c, 0:TH], ALU.add)
                ins.then_inc(xk_ready[layer], 1)

            def square(b, layer, i):
                e.wait_ge(emptied[("hidden", layer)], b * 4 + i + 1)
                hid = xk[:, i % 2, :]
                e.tensor_tensor(hid, hid, hid, ALU.mult).then_inc(hidden_ready[layer], 1)

            def add_value(b, layer, i):
                X = XA if layer == 0 else XB
                two, gates = slice(2 * (i % 2), 2 * (i % 2) + 2), xr[:, i % 2, :].rearrange("p (t d) -> p t d", d=D)
                e.wait_ge(emptied[("value", layer)], b * 4 + i + 1)
                e.tensor_tensor(upd[:, two, :], upd[:, two, :], gates, ALU.mult).then_inc(gated[layer], 1)
                e.wait_ge(gated[layer], b * 4 + i + 1)
                e.tensor_tensor(X[:, 2 * i:2 * i + 2, :], X[:, 2 * i:2 * i + 2, :], upd[:, two, :],
                                   ALU.add).then_inc(x_added[layer], 1)

            def add_output(b, t):
                if t == 0:
                    e.wait_ge(x1_loaded, b * 16 + 16)
                e.wait_ge(emptied["out"], b * 4 + t + 1)
                at = 2 * (t % 2)
                e.tensor_tensor(XB[:, 2 * t:2 * t + 2, :], XB[:, 2 * t:2 * t + 2, :], upd[:, at:at + 2, :],
                                   ALU.add).then_inc(out_added, 1)

            def later_parts(b, i):
                g, w, m = i // 4, i // 2 % 2, i % 2
                at = slice(TH * g, TH * (g + 1))
                e.wait_ge(emptied["qk"], b * 8 + i + 1)
                e.tensor_tensor(part[w][1][:, m, at], whole[:, i % 2, :], part[w][0][:, m, at], ALU.subtract)
                e.tensor_tensor(whole[:, i % 2, :], whole[:, i % 2, :], part[w][0][:, m, at],
                                   ALU.subtract).then_inc(rest_ready, 1)
                e.wait_ge(rest_ready, b * 8 + i + 1)
                e.tensor_tensor(part[w][2][:, m, at], whole[:, i % 2, :], part[w][1][:, m, at],
                                   ALU.subtract).then_inc(lo_ready, 1)

            def stage(what, a, c, b):
                if what == "mix":
                    mix(b, a, c)
                elif what == "hidden":
                    square(b, a, c)
                elif what == "value":
                    add_value(b, a, c)
                elif what == "out":
                    add_output(b, a)
                elif what == "qk":
                    later_parts(b, a)

            return stage

        @block.sync
        def _(sp):
            for t, src in ((w_sb["r"], wr), (w_sb["k"], wk), (w_sb["v"], wv), (w_sb["q"], wq),
                           (w_sb["kk"], wkk), (w_sb["vv"], wvv)):
                sp.dma_start(t[:, :, :], src).then_inc(w_loaded, 16)
            sp.dma_start(mu_sb[:, 0, :], mur).then_inc(w_loaded, 16)
            sp.dma_start(mu_sb[:, 1, :], muk).then_inc(w_loaded, 16)
            sp.wait_ge(pads_zero, 1)
            for h in range(UH):
                sp.dma_start(wo_sb[32 * h:32 * h + HD, :, :], wo[:, h, :, :]).then_inc(w_loaded, 16)

            sp.sem_inc(x_stored, 16)

            def batch_of(dram, b):
                return dram[b] if isinstance(b, int) else dram[bass.ds(b, 1)].rearrange("o p t d -> p (o t) d")

            def scratch(b):
                flat = x1[b] if isinstance(b, int) else x1[bass.ds(b, 1)].rearrange("o p n -> p (o n)")
                return flat.rearrange("p (t d) -> p t d", d=D)

            def load_x(b):
                sp.dma_start(XA[:, :, :], batch_of(x_v, b)).then_inc(x_loaded, 16)

            def save_x1(b):
                sp.wait_ge(x_added[0], b * 4 + 4)
                apart(sp)
                sp.dma_start(scratch(b), XA[:, :, :].rearrange("p t d -> p (t d)").rearrange("p (t d) -> p t d", d=D)
                             ).then_inc(x1_saved, 16)

            def load_stack(b, u):
                sp.wait_ge(lo_ready, b * 8 + 8)
                apart(sp)
                if counted(b * UNITS + u - 1):
                    sp.wait_ge(unit_scored, b * UNITS + u - 1)
                apart(sp)
                rows = slice(64 * (u % 2), 64 * (u % 2) + 64)
                for w, parts in ((0, QPART), (1, KPART)):
                    for j, i in enumerate(parts):
                        sp.dma_start(stack[w][u % 2][HD * j:HD * (j + 1), :, :],
                                     part[w][i][rows, u // 2, :]).then_inc(stack_loaded[u % 2], 16)

            def load_tau(b, u):
                sp.wait_ge(emptied["tau"], b * UNITS + u + 1)
                sp.dma_start(stack[0][u % 2][SROWS:TROWS, :, :], tauT[:, :]).then_inc(tau_loaded, 16)

            def store(b):
                sp.wait_ge(x_added[2], b * 4 + 4)
                apart(sp)
                sp.dma_start(batch_of(out_v, b), XB[:, :, :]).then_inc(x_stored, 16)

            def load_x1(b):
                sp.wait_ge(x_stored, b * 16 + 16)
                apart(sp)
                sp.wait_ge(x1_saved, b * 16 + 16)
                apart(sp)
                sp.dma_start(XB[:, :, :], scratch(b)).then_inc(x1_loaded, 16)

            def body(b, has_prev, has_next):
                at = schedule(has_prev, has_next)
                for pos in range(POSITIONS):
                    if pos == 3 and has_prev:
                        load_x1(b - 1)
                    for what, a, c, rel in at[pos]:
                        if what == "tau":
                            load_tau(b + rel, a)
                    if pos % 16 == 13 and pos < POSITIONS - 16:
                        load_stack(b, pos // 16 + 1)
                    if pos == 32 and has_next:
                        save_x1(b + 1)
                    if pos == 54 and has_prev:
                        store(b - 1)
                    if pos == 51 and has_next and (not isinstance(b, int) or b + 2 < BATCH):
                        sp.wait_ge(x1_saved, b * 16 + 32)
                        apart(sp)
                        sp.wait_ge(y_ready[1], (b + 1) * NT + NT)
                        apart(sp)
                        load_x(b + 2)
                    if pos == 61 and has_next:
                        load_stack(b + 1, 0)

            load_x(0)
            save_x1(0)
            sp.wait_ge(x1_saved, 16)
            sp.wait_ge(y_ready[1], NT)
            load_x(1)
            load_stack(0, 0)
            body(0, False, True)
            with sp.Fori(1, BATCH - 2) as b:
                body(b, True, True)
            body(BATCH - 2, True, True)
            body(BATCH - 1, True, False)
            load_x1(BATCH - 1)
            load_tau(BATCH - 1, UNITS - 1)
            store(BATCH - 1)
            sp.wait_ge(x_stored, BATCH * 16 + 16)

        @block.gpsimd
        def _(pool):
            pool.memset(wo_sb[:, :, :], 0.0).then_inc(pads_zero, 1)
            pool.memset(ident[:, :], 0.0).then_inc(const_chain, 1)
            pool.memset(ident_b[:, :], 0.0).then_inc(const_chain, 1)
            pool.memset(mask_row[:, :], 0.0).then_inc(const_chain, 1)
            pool.memset(mask_col[:, :], 0.0).then_inc(const_chain, 1)
            pool.memset(carry[:, :, :], 1.0).then_inc(const_chain, 1)
            pool.memset(eps_sb[:, :], EPS)
            pool.memset(zero_sb[:, :], 0.0)
            pool.memset(n_square[:, :], 0.0)
            for r in range(TOP):
                pool.memset(inv_rank[:, :, r:r + 1], 1.0 / (r + 1))
            pool.wait_ge(const_chain, 5)
            for t in (ident, ident_b):
                pool.affine_select(out=t[:, :], in_=t[:, :], compare_op=ALU.not_equal, fill=1.0, base=0,
                                   pattern=[[-1, P]], channel_multiplier=1)
            pool.affine_select(out=mask_row[:, :], in_=mask_row[:, :], compare_op=ALU.is_ge, fill=MASKED, base=0,
                               pattern=[[-1, P]], channel_multiplier=1)
            pool.affine_select(out=mask_col[:, :], in_=mask_col[:, :], compare_op=ALU.is_ge, fill=MASKED, base=0,
                               pattern=[[1, P]], channel_multiplier=-1)
            pool.memset(carry[:, :, 0:1], 0.0)
            pool.drain().then_inc(consts, 1)
            pool.wait_ge(w_loaded, 12 * 16)

            def join_flags(b, n):
                pool.wait_ge(flags_ready, b * PUS + n + 1)
                apart(pool)
                pool.partition_all_reduce(flag_all[:, n % 2, :], flag[:, n % 2, :], P,
                                          bass.bass_isa.ReduceOp.max).then_inc(flags_joined, 1)

            def split(b, u):
                pool.wait_ge(pu_settled, b * PUS + PAIRS * (u + 1))
                apart(pool)
                if counted(b * UNITS + u):
                    pool.wait_ge(filled["tau"], b * UNITS + u)
                apart(pool)
                t = tau[u % 2][:, :, :].rearrange("p h q -> p (h q)")
                base = b * UNITS * 5 + 5 * u

                def after(k):
                    pool.wait_ge(split_chain, base + k)
                    apart(pool)

                pool.tensor_scalar(ntau[:, 0, :], t, -1.0, 0.0, ALU.mult, ALU.add).then_inc(split_chain, 1)
                after(1)
                pool.tensor_copy(tau_part[:, 0, :], ntau[:, 0, :]).then_inc(split_chain, 1)
                after(2)
                pool.tensor_tensor(ntau[:, 1, :], ntau[:, 0, :], tau_part[:, 0, :], ALU.subtract).then_inc(split_chain, 1)
                after(3)
                pool.tensor_copy(tau_part[:, 1, :], ntau[:, 1, :]).then_inc(split_chain, 1)
                after(4)
                pool.tensor_tensor(tau_part[:, 2, :], ntau[:, 1, :], tau_part[:, 1, :], ALU.subtract).then_inc(split_chain, 1)
                after(5)
                pool.sem_inc(tau_split, 1)

            token_stage = token_work(pool)

            def body(b, has_prev, has_next):
                at = schedule(has_prev, has_next)
                for pos in range(POSITIONS):
                    if pos % UH == settle_at(pos // UH) and pos >= UH:
                        join_flags(b, pos // UH - 1)
                    elif pos == settle_at(0) and has_prev:
                        join_flags(b - 1, PUS - 1)
                    for what, a, c, rel in at[pos]:
                        if what == "split":
                            split(b + rel, a)
                        else:
                            token_stage(what, a, c, b + rel)

            def behind():
                join_flags(BATCH - 1, PUS - 1)
                split(BATCH - 1, UNITS - 1)

            batches(pool, lambda: None, body, behind)

        @block.tensor
        def _(pe):
            pe.wait_ge(w_loaded, 12 * 16)
            pe.wait_ge(consts, 1)
            pe.wait_ge(psum_zeroed, 1)
            ring = {"next": 0}
            last_use = {}

            def open_bank(semaphore, per_batch, b, i):
                at = ring["next"]
                if at in last_use:
                    semaphore_then, per_batch_then, b_then, i_then = last_use[at]
                    pe.wait_ge(semaphore_then, b_then * per_batch_then + (i_then + 1))
                last_use[at] = (semaphore, per_batch, b, i)
                ring["next"] = (at + 1) % BANKS
                return bank_ps[:, at, :]

            def open_task(kind, b, i):
                return open_bank(emptied[kind], KINDS[kind], b, i)

            def product(m, left, right):
                for c in range(len(left)):
                    ins = pe.matmul(m, left[c], right[c], start=(c == 0), stop=(c == len(left) - 1))
                return ins

            def turn(b, layer, i):
                g, c = divmod(i, C)
                pe.wait_ge(y_ready[layer], b * NT + 4 * g + 4)
                m = open_task(("yT", layer), b, i)
                for t in range(4):
                    ins = pe.transpose(m[:, P * t:P * (t + 1)], ytok[:, t, P * c:P * (c + 1)], ident[:, :])
                ins.then_inc(filled[("yT", layer)], 1)

            def gate(b, layer, i):
                pe.wait_ge(xr_ready[layer], b * G + i // 2 + 1)
                m = open_task(("gate", layer), b, i)
                for t in range(2):
                    at = P * (2 * (i % 2) + t)
                    ins = product(m[:, D * t:D * (t + 1)], [xr[:, c, at:at + P] for c in range(C)],
                                  [w_sb["r"][:, c, :] for c in range(C)])
                ins.then_inc(filled[("gate", layer)], 1)

            def hidden(b, layer, i):
                mm = i % 2
                pe.wait_ge(xk_ready[layer], b * G + i // 2 + 1)
                m = open_task(("hidden", layer), b, i)
                product(m, [w_sb["k"][:, c, P * mm:P * (mm + 1)] for c in range(C)],
                        [xk[:, c, :] for c in range(C)]).then_inc(filled[("hidden", layer)], 1)

            def value(b, layer, i):
                pe.wait_ge(hidden_ready[layer], b * 4 + 2 * (i // 2) + 2)
                m = open_task(("value", layer), b, i)
                for t in range(2):
                    at = P * (2 * (i % 2) + t)
                    ins = product(m[:, D * t:D * (t + 1)], [xk[:, c, at:at + P] for c in range(C)],
                                  [w_sb["v"][:, c, :] for c in range(C)])
                ins.then_inc(filled[("value", layer)], 1)

            def project(b, i):
                g, w, mm = i // 4, i // 2 % 2, i % 2
                pe.wait_ge(emptied[("yT", 1)], b * 4 + 2 * g + 2)
                m = open_task("qk", b, i)
                name = ("q", "kk")[w]
                product(m, [w_sb[name][:, c, P * mm:P * (mm + 1)] for c in range(C)],
                        [y2T[:, c, TH * g:TH * (g + 1)] for c in range(C)]).then_inc(filled["qk"], 1)

            def values(b, t):
                m = open_task("val", b, t)
                for i in range(2):
                    at = P * (2 * t + i)
                    ins = product(m[:, D * i:D * (i + 1)], [y2T[:, c, at:at + P] for c in range(C)],
                                  [w_sb["vv"][:, c, :] for c in range(C)])
                ins.then_inc(filled["val"], 1)

            def outputs(b, t):
                pe.wait_ge(o_copied, b * 8 + 8)
                m = open_task("out", b, t)
                for i in range(2):
                    at = P * (2 * t + i)
                    ins = product(m[:, D * i:D * (i + 1)], [OT[:, u, at:at + P] for u in range(UNITS)],
                                  [wo_sb[:, u, :] for u in range(UNITS)])
                ins.then_inc(filled["out"], 1)

            def turn_tau(b, u):
                m = open_task("tau", b, u).bitcast(BF16)
                pe.wait_ge(tau_split, b * UNITS + u + 1)
                pe.transpose(m[0:3 * UH * NT, 0:P], tau_part[:, :, :].rearrange("p a q -> p (a q)"),
                             ident_b[:, :]).then_inc(filled["tau"], 1)

            def scores_head(b, n, hh):
                u, p = n // PAIRS, n % PAIRS
                q, k = stack[0][u % 2], stack[1][u % 2]
                if n % PAIRS == 0 and hh == 0:
                    pe.wait_ge(stack_loaded[u % 2], b * 384 + 192 * (u // 2 + 1))
                for i, (qt, a, w, _) in enumerate(row_chunks(p)):
                    at = PU_ROWS * n + CHUNKS * hh + i
                    bank = open_bank(row_copied, PU_ROWS * PUS, b, at)
                    last = a + w == (qt + 1) * P
                    ins = pe.matmul(bank[:, 0:w], q[0:SROWS, hh, P * qt:P * (qt + 1)], k[0:SROWS, hh, a:a + w],
                                    start=True, stop=not last)
                    if last:
                        ins = pe.matmul(bank[:, w - P:w], ident_b[:, :], mask_row[:, :], start=False, stop=True)
                    ins.then_inc(row_filled, 1)

            def step_scores(b, u, k):
                s, j, q0 = STEPS[k]
                w = TH * (s + 1) - q0
                q, kk = stack[0][u % 2], stack[1][u % 2]
                if k == 0:
                    pe.wait_ge(tau_loaded, b * 64 + 16 * (u + 1))
                diagonal = P * j >= TH * s
                for hh in range(UH):
                    m = open_bank(probs_ready[hh], UNITS * len(STEPS), b, len(STEPS) * u + k)
                    ins = pe.matmul(m[:, 0:w], kk[0:TROWS, hh, P * j:P * (j + 1)], q[0:TROWS, hh, q0:q0 + w],
                                    start=True, stop=not diagonal)
                    if diagonal:
                        ins = pe.matmul(m[:, 0:P], ident_b[:, :], mask_col[:, :], start=False, stop=True)
                    ins.then_inc(col_filled, 1)
                if k == len(STEPS) - 1:
                    pe.wait_ge(col_filled, b * UNITS * UNIT_BLOCKS + UNIT_BLOCKS * (u + 1))
                    pe.sem_inc(unit_scored, 1)

            def step_values(b, u, k):
                s, j, q0 = STEPS[k]
                w = TH * (s + 1) - q0
                if j == 0:
                    if counted(b * 8 + 2 * u + s):
                        pe.wait_ge(o_copied, b * 8 + 2 * u + s)
                    if u == 0 and s == 0:
                        pe.wait_ge(emptied["val"], b * 4 + 4)
                for hh in range(UH):
                    pe.wait_ge(probs_ready[hh], b * UNITS * len(STEPS) + len(STEPS) * u + k + 1)
                    col = (UH * u + hh) * HD
                    ins = pe.matmul(o_ps[32 * hh:32 * hh + HD, TH - w:TH], V[:, j, col:col + HD],
                                    probs[:, k % 2, hh, 0:w], start=(j == 0), stop=(P * (j + 1) == TH * (s + 1)),
                                    skip_group_check=True)
                ins.then_inc(pv_done, 1)

            def second_pass(b, u, steps):
                for k in steps:
                    if k < len(STEPS):
                        step_scores(b, u, k)
                    if k:
                        step_values(b, u, k - 1)

            STAGES = {"turn": turn, "gate": gate, "hidden": hidden, "value": value}

            def stage(what, a, c, b):
                if what in STAGES:
                    STAGES[what](b, a, c)
                elif what == "qk":
                    project(b, a)
                elif what == "val":
                    values(b, a)
                elif what == "out":
                    outputs(b, a)
                elif what == "tau":
                    turn_tau(b, a)

            def before():
                for e in BEFORE:
                    stage(*e)

            def body(b, has_prev, has_next):
                ring["next"] = first_bank(has_prev, has_next)
                if has_prev:
                    for at, (semaphore, per_batch, _, i) in last_use.items():
                        last_use[at] = (semaphore, per_batch, b, i - per_batch)
                at = schedule(has_prev, has_next)
                for pos in range(POSITIONS):
                    n, hh = divmod(pos, UH)
                    scores_head(b, n, hh)
                    for what, a, c, rel in at[pos]:
                        stage(what, a, c, b + rel)
                    u, steps = steps_at(pos)
                    if u >= 0 or has_prev:
                        second_pass(b if u >= 0 else b - 1, u % UNITS, steps)

            def behind():
                b = BATCH - 1
                turn_tau(b, UNITS - 1)
                second_pass(b, UNITS - 1, range(len(STEPS) + 1))
                for e in BEHIND_LAST:
                    stage(*e)

            batches(pe, before, body, behind)

        @block.scalar
        def _(act):
            act.wait_ge(consts, 1)
            ring = {"next": 0}

            def root(b, layer):
                act.wait_ge(stats_ready[layer], b + 1)
                act.activation(sd[layer][:, :], mv[layer][:, :, 1], ACT.Sqrt, bias=eps_sb[:, 0:1]).then_inc(sd_ready[layer], 1)

            def normalise(b, layer, g):
                X = XB if layer == 2 else XA
                act.wait_ge(scale_ready[layer], b + 1)
                for t in range(4):
                    at = 4 * g + t
                    act.activation(ytok[:, t, :], X[:, at, :], ACT.Identity, bias=shift[layer][:, at:at + 1],
                                   scale=rstd[layer][:, at:at + 1]).then_inc(y_ready[layer], 1)

            def last_unit(b):
                return min(b + 2, BATCH - 1) if isinstance(b, int) else b + 2

            def turned(b, layer, i):
                g, c = divmod(i, C)
                act.wait_ge(filled[("yT", layer)], b * 4 + i + 1)
                m = bank_ps[:, bank(), :]
                if layer == 1:
                    act.activation(y2T[:, c, TH * g:TH * (g + 1)], m, ACT.Copy).then_inc(emptied[("yT", 1)], 1)
                    return
                if g == 1:
                    act.wait_ge(xk_ready[layer], b * G + 1)
                if c == 0:
                    act.activation(yT[:, :, 0], zero_sb[:, :] if g == 0 else yT[:, :, TH], ACT.Copy)
                    act.drain()
                act.activation(yT[:, c, 1:TH + 1], m, ACT.Copy).then_inc(emptied[("yT", layer)], 1)

            def two_tiles(t):
                return bank_ps[:, bank(), :].rearrange("p (t d) -> p t d", d=D), slice(2 * t, 2 * t + 2)

            def gates(b, layer, i):
                if i % 2 == 0:
                    return
                act.wait_ge(filled[("gate", layer)], b * 4 + i + 1)
                for t in range(2):
                    act.activation(xr[:, t, :], bank_ps[:, bank(), :], ACT.Sigmoid).then_inc(emptied[("gate", layer)], 1)

            def hidden(b, layer, i):
                if i % 2 == 0:
                    return
                act.wait_ge(filled[("hidden", layer)], b * 4 + i + 1)
                for t in range(2):
                    act.activation(xk[:, t, :], bank_ps[:, bank(), :], ACT.Relu).then_inc(emptied[("hidden", layer)], 1)

            def value(b, layer, i):
                if layer == 0 and i == 0 and counted(b - 1):
                    act.wait_ge(x_stored, b * 16 - 16)
                elif layer == 0 and i == 2:
                    act.wait_ge(x_added[0], b * 4 + 2)
                    if counted(b - 1):
                        act.wait_ge(out_added, b * 4 - 4)
                elif layer == 2 and i == 0:
                    act.wait_ge(x_added[0], last_unit(b) * 4 + 4)
                elif layer == 2 and i == 2:
                    act.wait_ge(x_added[2], b * 4 + 2)
                act.wait_ge(filled[("value", layer)], b * 4 + i + 1)
                m, two = two_tiles(i % 2)
                act.activation(upd[:, two, :], m, ACT.Copy, scale=0.5).then_inc(emptied[("value", layer)], 1)

            def output(b, t):
                if t == 0:
                    act.wait_ge(x1_loaded, b * 16 + 16)
                    act.wait_ge(x_added[0], last_unit(b) * 4 + 2)
                elif t >= 2:
                    act.wait_ge(out_added, b * 4 + t - 1)
                act.wait_ge(filled["out"], b * 4 + t + 1)
                m, two = two_tiles(t % 2)
                act.activation(upd[:, two, :], m, ACT.Copy).then_inc(emptied["out"], 1)

            def parts(b, i):
                g, w, m = i // 4, i // 2 % 2, i % 2
                if i == 0 and counted(b):
                    act.wait_ge(stack_loaded[1], b * 384)
                if counted(b * 8 + i - 1):
                    act.wait_ge(lo_ready, b * 8 + i - 1)
                act.wait_ge(filled["qk"], b * 8 + i + 1)
                scale, bk = (0.25 if w == 0 else 1.0), bank()
                act.activation(whole[:, i % 2, :], bank_ps[:, bk, :], ACT.Copy, scale=scale)
                act.activation(part[w][0][:, m, TH * g:TH * (g + 1)], bank_ps[:, bk, :], ACT.Copy,
                               scale=scale).then_inc(emptied["qk"], 1)

            def values(b, t):
                act.wait_ge(filled["val"], b * 4 + t + 1)
                m, two = two_tiles(t)
                act.activation(V[:, two, :], m, ACT.Copy).then_inc(emptied["val"], 1)

            def turned_tau(b, u):
                act.wait_ge(filled["tau"], b * UNITS + u + 1)
                if counted(b * 64 + 16 * u):
                    act.wait_ge(tau_loaded, b * 64 + 16 * u)
                act.activation(tauT[:, :], bank_ps[:, bank(), :].bitcast(BF16)[0:3 * UH * NT, 0:P],
                               ACT.Copy).then_inc(emptied["tau"], 1)

            def copy_head(b, n, hh):
                if hh == 0:
                    if counted(b * PUS + n - 1):
                        act.wait_ge(pu_settled, b * PUS + n - 1)
                for i, (qt, a, w, place) in enumerate(row_chunks(n % PAIRS)):
                    at = PU_ROWS * n + CHUNKS * hh + i
                    act.wait_ge(row_filled, b * PU_ROWS * PUS + at + 1)
                    act.activation(score[n % 2][:, hh, place:place + w], bank_ps[:, bank(), 0:w],
                                   ACT.Copy).then_inc(row_copied, 1)

            def step_probs(b, u, k):
                s, j, q0 = STEPS[k]
                w = TH * (s + 1) - q0
                if counted(b * 48 + 12 * u + k - 1):
                    act.wait_ge(pv_done, b * 48 + 12 * u + k - 1)
                for hh in range(UH):
                    at = UNIT_BLOCKS * u + UH * k + hh
                    act.wait_ge(col_filled, b * UNITS * UNIT_BLOCKS + at + 1)
                    act.activation(probs[:, k % 2, hh, 0:w], bank_ps[:, bank(), 0:w], ACT.Relu).then_inc(probs_ready[hh], 1)

            def output_half(b, u, s):
                act.wait_ge(pv_done, b * 48 + 12 * u + (4 if s == 0 else 12))
                if u == 0 and s == 0:
                    if counted(b * 8):
                        act.wait_ge(filled["out"], b * 4)
                act.activation(OT[:, u, TH * s:TH * (s + 1)], o_ps[:, :], ACT.Copy).then_inc(o_copied, 1)

            def second_pass(b, u, steps):
                for k in steps:
                    if k < len(STEPS):
                        step_probs(b, u, k)
                    if k == 4:
                        output_half(b, u, 0)
                    if k == len(STEPS):
                        output_half(b, u, 1)

            def bank():
                at = ring["next"]
                ring["next"] = (at + 1) % BANKS
                return at

            def stage(what, a, c, b):
                if what == "root":
                    root(b, a)
                elif what == "norm":
                    normalise(b, a, c)
                elif what == "turn":
                    turned(b, a, c)
                elif what == "gate":
                    gates(b, a, c)
                elif what == "hidden":
                    hidden(b, a, c)
                elif what == "value":
                    value(b, a, c)
                elif what == "qk":
                    parts(b, a)
                elif what == "val":
                    values(b, a)
                elif what == "out":
                    output(b, a)
                elif what == "tau":
                    turned_tau(b, a)

            def before():
                for e in BEFORE:
                    stage(*e)

            def body(b, has_prev, has_next):
                ring["next"] = first_bank(has_prev, has_next)
                at = schedule(has_prev, has_next)
                for pos in range(POSITIONS):
                    n, hh = divmod(pos, UH)
                    copy_head(b, n, hh)
                    for what, a, c, rel in at[pos]:
                        stage(what, a, c, b + rel)
                    u, steps = steps_at(pos)
                    if u >= 0 or has_prev:
                        second_pass(b if u >= 0 else b - 1, u % UNITS, steps)

            def behind():
                b = BATCH - 1
                turned_tau(b, UNITS - 1)
                second_pass(b, UNITS - 1, range(len(STEPS) + 1))
                for e in BEHIND_LAST:
                    stage(*e)

            batches(act, before, body, behind)

        @block.vector
        def _(dve):
            for i in range(2):
                dve.memset(stack[1][i][SROWS:TROWS, :, :], 1.0)
            dve.memset(o_ps[:, :], 0.0).then_inc(psum_zeroed, 1)
            dve.wait_ge(consts, 1)
            dve.wait_ge(w_loaded, 12 * 16)

            def statistics(b, layer):
                X = XB if layer == 2 else XA
                if layer == 0:
                    dve.wait_ge(x_loaded, b * 16 + 16)
                elif layer == 1:
                    dve.wait_ge(x_added[0], b * 4 + 4)
                else:
                    dve.wait_ge(out_added, b * 4 + 4)
                for t in range(NT):
                    ins = dve.bn_stats(stats[:, t, :], X[:, t, :])
                ins.then_inc(ln_chain[layer], 1)
                dve.wait_ge(ln_chain[layer], b * 3 + 1)
                apart(dve)
                for t in range(NT):
                    ins = dve.bn_aggr(mv[layer][:, t, :], stats[:, t, :])
                ins.then_inc(stats_ready[layer], 1)

            def scale(b, layer):
                dve.wait_ge(sd_ready[layer], b + 1)
                dve.reciprocal(rstd[layer][:, :], sd[layer][:, :]).then_inc(ln_chain[layer], 1)
                dve.wait_ge(ln_chain[layer], b * 3 + 2)
                dve.scalar_tensor_tensor(out=shift[layer][:, :], in0=mv[layer][:, :, 0], scalar=-1.0, in1=rstd[layer][:, :],
                                         op0=ALU.mult, op1=ALU.mult).then_inc(ln_chain[layer], 1)
                dve.wait_ge(ln_chain[layer], b * 3 + 3)
                dve.sem_inc(scale_ready[layer], 1)

            def first_eights(b, n, hh):
                p = n % PAIRS
                dve.wait_ge(row_copied, b * PU_ROWS * PUS + PU_ROWS * n + CHUNKS * (hh + 1))
                apart(dve)
                for i, (qt, base) in enumerate(((p, 0), (NT - 1 - p, (p + 1) * P))):
                    for k in range(RUNS):
                        last = dve.max(cand[:, 2 * hh + i, 8 * k:8 * k + 8],
                                       score[n % 2][:, hh, base + k:base + (qt + 1) * P:RUNS])
                return last

            def thresholds(b, n, last):
                u, p = n // PAIRS, n % PAIRS
                count = [b * THR_STEPS + THR_PU * n]
                done = [0]

                def link(ins):
                    done[0] += 1
                    ins.then_inc(thr_chain, 1)

                def after(back=0):
                    dve.wait_ge(thr_chain, count[0] + done[0] - back)

                edge2 = edge[:, :, :].rearrange("p h a -> p (h a)")
                link(last)
                after()
                apart(dve)
                for h in range(HT):
                    last = dve.max(best[:, h, 0:8], cand[:, h, :])
                link(last)
                link(dve.tensor_reduce(edge2, cand[:, :, 7:CAND:8], AX.X, ALU.max))
                after(1)
                apart(dve)
                for h in range(HT):
                    last = dve.match_replace(rest[:, h, :], best[:, h, 0:8], cand[:, h, :], MASKED)
                link(last)
                after()
                apart(dve)
                for h in range(HT):
                    last = dve.max(best[:, h, 8:16], rest[:, h, :])
                link(last)
                after()
                link(dve.tensor_tensor_scan(cum[:, :, :].rearrange("p h r -> p (h r)"),
                                            carry[:, :, :].rearrange("p h r -> p (h r)"),
                                            best[:, :, :].rearrange("p h r -> p (h r)"), 0.0, ALU.mult, ALU.add))
                link(dve.tensor_tensor(edge2, edge2, best[:, :, TOP - 1], ALU.max))
                after(1)
                link(dve.scalar_tensor_tensor(out=cum[:, :, :], in0=cum[:, :, :], scalar=-1.0, in1=inv_rank[:, :, :],
                                              op0=ALU.add, op1=ALU.mult))
                if counted(b * UNITS + u - 1):
                    dve.wait_ge(tau_split, b * UNITS + u - 1)
                after()
                t = tau[u % 2][:, :, p:NT - p:NT - 1 - 2 * p]
                link(dve.tensor_reduce(t, cum[:, :, :].rearrange("p (h a) r -> p h a r", a=2), AX.X, ALU.max))
                after()
                mine = flag[:, n % 2, :]
                link(dve.tensor_tensor(mine[:, 0:HT].rearrange("p (h a) -> p h a", a=2), edge[:, :, :], t, ALU.is_gt))
                after()
                dve.tensor_reduce(mine[:, HT:HT + 1], mine[:, 0:HT], AX.X, ALU.max).then_inc(flags_ready, 1)
                assert done[0] == THR_PU, done[0]

            def settle(b, n):
                u, p = n // PAIRS, n % PAIRS
                dve.wait_ge(flags_joined, b * PUS + n + 1)
                apart(dve)
                joined = flag_all[0:1, n % 2, :].bitcast(I32)
                flagged = dve.value_load(joined[:, HT:HT + 1])
                with dve.If(flagged > 0):
                    for i, (qt, base) in enumerate(((p, 0), (NT - 1 - p, (p + 1) * P))):
                        width = (qt + 1) * P
                        with dve.Fori(0, UH) as hh:
                            left = dve.value_load(joined[:, bass.ds(2 * hh + i, 1)])
                            with dve.If(left > 0):
                                scores = score[n % 2][:, bass.ds(hh, 1), base:base + width].rearrange("p o k -> p (o k)")
                                newton(scores, tau[u % 2][:, bass.ds(hh, 1), qt], width)
                dve.drain().then_inc(pu_settled, 1)

            def newton_steps(scores, width, steps):
                for i in range(steps):
                    dve.scalar_tensor_tensor(out=junk[:, 0:width], in0=scores, scalar=n_tau[:, 0:1], in1=scores,
                                             op0=ALU.is_gt, op1=ALU.mult, accum_out=n_sum[:, :])
                    dve.drain()
                    dve.tensor_scalar(junk[:, 0:width], scores, n_tau[:, 0:1], 0.0, ALU.is_gt, ALU.add,
                                      accum_out=n_cnt[:, i % 2:i % 2 + 1])
                    dve.drain()
                    dve.tensor_scalar(n_inv[:, :], n_cnt[:, i % 2:i % 2 + 1], 1.0, None, ALU.max)
                    dve.drain()
                    dve.reciprocal(n_inv[:, :], n_inv[:, :])
                    dve.drain()
                    dve.tensor_scalar(n_tau[:, :], n_sum[:, :], -1.0, n_inv[:, 0:1], ALU.add, ALU.mult)
                    dve.drain()
                dve.tensor_tensor(n_square[:, 0:1], n_cnt[:, 0:1], n_cnt[:, 1:2], ALU.not_equal)
                dve.drain()
                dve.transpose(n_turned[:, :], n_square[:, :])
                dve.drain()
                dve.tensor_reduce(n_left[:, :], n_turned[:, :], AX.X, ALU.add)
                dve.drain()

            def rows_left():
                return (dve.value_load(n_left[0:1, 0:1]) + dve.value_load(n_left[32:33, 0:1])
                        + dve.value_load(n_left[64:65, 0:1]) + dve.value_load(n_left[96:97, 0:1]))

            def newton(scores, mine, width):
                dve.tensor_copy(n_tau[:, :], mine)
                dve.drain()
                newton_steps(scores, width, 3)
                with dve.If(rows_left() > 0):
                    with dve.Fori(0, ROUNDS):
                        with dve.If(rows_left() > 0):
                            newton_steps(scores, width, 2)
                dve.tensor_copy(mine, n_tau[:, :])
                dve.drain()

            def stage(what, a, c, b):
                if what == "stats":
                    statistics(b, a)
                elif what == "scale":
                    scale(b, a)

            token_stage = token_work(dve)

            def before():
                for e in BEFORE:
                    stage(*e)
                    token_stage(*e)

            def body(b, has_prev, has_next):
                at = schedule(has_prev, has_next)
                for pos in range(POSITIONS):
                    n, hh = divmod(pos, UH)
                    last = first_eights(b, n, hh)
                    if hh == settle_at(n) and n:
                        settle(b, n - 1)
                    elif hh == settle_at(n) and has_prev:
                        settle(b - 1, PUS - 1)
                    for what, a, c, rel in at[pos]:
                        stage(what, a, c, b + rel)
                    if hh == UH - 1:
                        thresholds(b, n, last)

            def behind():
                settle(BATCH - 1, PUS - 1)
                for e in BEHIND_LAST:
                    stage(*e)
                    token_stage(*e)

            batches(dve, before, body, behind)


def kernel(**inputs):
    import numpy as _np
    import concourse.bacc as _bacc
    from concourse import mybir as _mybir
    from concourse.bass_utils import run_bass_kernel_spmd as _run

    def rows(w):
        return _np.ascontiguousarray(w.T.reshape(C, P, D).transpose(1, 0, 2))

    def by_feature(w):
        return w.reshape(UNITS, UH, HD, D).transpose(0, 2, 1, 3).reshape(D, D)

    i = {k: _np.asarray(v) for k, v in inputs.items()}
    arrays = {
        "x": i["L0_attn_x"],
        "wr": rows(i["L0_ffn_W_r"]), "wk": rows(i["L0_ffn_W_k"]), "wv": rows(i["L0_ffn_W_v"]),
        "mur": i["L0_ffn_mu_r"].reshape(C, P).T, "muk": i["L0_ffn_mu_k"].reshape(C, P).T,
        "wq": rows(by_feature(i["L0_attn_Wq"])), "wkk": rows(by_feature(i["L0_attn_Wk"])),
        "wvv": rows(i["L0_attn_Wv"]),
        "wo": i["L0_attn_Wo"].T.reshape(UNITS, UH, HD, D).transpose(2, 1, 0, 3),
    }
    arrays = {f"in_{k}": _np.ascontiguousarray(v) for k, v in arrays.items()}
    nc = _bacc.Bacc("TRN2", target_bir_lowering=False, num_devices=1)
    args = [nc.dram_tensor(k, a.shape, _mybir.dt.from_np(a.dtype), kind="ExternalInput").ap()
            for k, a in arrays.items()]
    args.append(nc.dram_tensor("x1_scratch", (BATCH, P, NT * D), _mybir.dt.float32, kind="Internal").ap())
    args.append(nc.dram_tensor("out_dram", (BATCH, T, D), _mybir.dt.float32, kind="ExternalOutput").ap())
    macaron(nc, *args)
    r = _run(nc, [arrays], core_ids=[0])
    return r.results[0]["out_dram"]
```
